# Optimizing a Trainium2 kernel written in Bass

```python
import numpy as np
import jax
import jax.numpy as jnp

def _softmax(x, axis=-1):
    return jax.nn.softmax(x, axis=axis)

def _gelu(x):
    return jax.nn.gelu(x, approximate=True)

def _silu(x):
    return jax.nn.silu(x)

def _sigmoid(x):
    return jax.nn.sigmoid(x)

def _layernorm(x, axis=-1, eps=1e-05):
    m = jnp.mean(x, axis=axis, keepdims=True)
    v = jnp.var(x, axis=axis, keepdims=True)
    return (x - m) / jnp.sqrt(v + eps)

def _scatter_add(tgt, idx, src, axis=0):
    return tgt.at[idx].add(src)

def _segment_sum(src, seg, n):
    return jax.ops.segment_sum(src, seg, n)
kernel_name = 'mk_adaln_d1_jaxref_r8_fa9763'

def setup_inputs(seed: int=0):
    np.random.seed(seed)
    _w = jnp.asarray

    def _L0_attn_setup():
        import jax, jax.numpy as jnp
        import numpy as np
        import math
        B, S, DM, H, F = (2, 256, 128, 16, 192)
        DH = F // 3
        MAX_BIAS = 8.0

        def _get_slopes(n):

            def pow2(n):
                start = 2.0 ** (-2.0 ** (-(math.log2(n) - 3)))
                return [start * start ** i for i in range(n)]
            if math.log2(n).is_integer():
                return pow2(n)
            cp2 = 2 ** math.floor(math.log2(n))
            return pow2(cp2) + _get_slopes(2 * cp2)[0::2][:n - cp2]

        def _rope_sin_cos(seq_len, dim):
            inv_freq = 1.0 / 10000.0 ** (jnp.arange(0, dim, 2, dtype=jnp.float32) / dim)
            freqs = jnp.outer(jnp.arange(seq_len, dtype=jnp.float32), inv_freq)
            sin = jnp.concatenate([jnp.sin(freqs), jnp.sin(freqs)], axis=-1)
            cos = jnp.concatenate([jnp.cos(freqs), jnp.cos(freqs)], axis=-1)
            return (sin, cos)

        def _rotate_half(x):
            x1, x2 = jnp.split(x, 2, axis=-1)
            return jnp.concatenate([-x2, x1], axis=-1)
        key = jax.random.key(seed)
        kx, kq, ko = jax.random.split(key, 3)
        x = jax.random.normal(kx, (B, S, DM), dtype=jnp.float32)
        w_qkv = jax.random.normal(kq, (DM, H, F), dtype=jnp.float32) * (1.0 / math.sqrt(DM))
        b_qkv = jnp.zeros((H, F), dtype=jnp.float32)
        w_out = jax.random.normal(ko, (H, DH, DM), dtype=jnp.float32) * (1.0 / math.sqrt(H * DH))
        b_out = jnp.zeros((DM,), dtype=jnp.float32)
        return {'x': x, 'w_qkv': w_qkv, 'b_qkv': b_qkv, 'w_out': w_out, 'b_out': b_out}
    _L0_attn_in = _L0_attn_setup()

    def _L0_ffn_setup():
        import jax, jax.numpy as jnp
        import numpy as np
        B, S, D, H, E = (4, 256, 128, 512, 8)
        THRESHOLD = 0.5
        key = jax.random.key(seed)
        ks = jax.random.split(key, 7)
        s_in = 1.0 / np.sqrt(D)
        s_h = 1.0 / np.sqrt(H)
        return {'x': jax.random.normal(ks[0], (B, S, D), dtype=jnp.float32), 'Wg': jax.random.uniform(ks[1], (D, E), jnp.float32, -s_in, s_in), 'bg': jax.random.uniform(ks[2], (E,), jnp.float32, -s_in, s_in), 'W1': jax.random.uniform(ks[3], (E, D, H), jnp.float32, -s_in, s_in), 'b1': jax.random.uniform(ks[4], (E, H), jnp.float32, -s_in, s_in), 'W2': jax.random.uniform(ks[5], (E, H, D), jnp.float32, -s_h, s_h), 'b2': jax.random.uniform(ks[6], (E, D), jnp.float32, -s_h, s_h)}
    _L0_ffn_in = _L0_ffn_setup()
    _L0_c = _w((lambda *s: np.random.randn(*s).astype(np.float32) * 0.05)(1, 128))
    _L0_wmod = _w((lambda *s: np.random.randn(*s).astype(np.float32) * 0.05)(128, 6 * 128) * 128 ** (-0.5))
    _d = {'L0_attn_x': _L0_attn_in['x'], 'L0_attn_w_qkv': _L0_attn_in['w_qkv'], 'L0_attn_b_qkv': _L0_attn_in['b_qkv'], 'L0_attn_w_out': _L0_attn_in['w_out'], 'L0_attn_b_out': _L0_attn_in['b_out'], 'L0_ffn_Wg': _L0_ffn_in['Wg'], 'L0_ffn_bg': _L0_ffn_in['bg'], 'L0_ffn_W1': _L0_ffn_in['W1'], 'L0_ffn_b1': _L0_ffn_in['b1'], 'L0_ffn_W2': _L0_ffn_in['W2'], 'L0_ffn_b2': _L0_ffn_in['b2'], 'L0_c': _L0_c, 'L0_wmod': _L0_wmod}
    _x0 = _d['L0_attn_x']
    _d['L0_attn_x'] = jax.random.normal(jax.random.fold_in(jax.random.key(seed), 1), (1, 2048, 128), dtype=_x0.dtype)
    del _x0
    return _d

def reference(L0_attn_x, L0_attn_w_qkv, L0_attn_b_qkv, L0_attn_w_out, L0_attn_b_out, L0_ffn_Wg, L0_ffn_bg, L0_ffn_W1, L0_ffn_b1, L0_ffn_W2, L0_ffn_b2, L0_c, L0_wmod):

    def _L0_attn_ref(x, w_qkv, b_qkv, w_out, b_out):
        import jax, jax.numpy as jnp
        import numpy as np
        import math
        B, S, DM, H, F = (2, 256, 128, 16, 192)
        DH = F // 3
        MAX_BIAS = 8.0

        def _get_slopes(n):

            def pow2(n):
                start = 2.0 ** (-2.0 ** (-(math.log2(n) - 3)))
                return [start * start ** i for i in range(n)]
            if math.log2(n).is_integer():
                return pow2(n)
            cp2 = 2 ** math.floor(math.log2(n))
            return pow2(cp2) + _get_slopes(2 * cp2)[0::2][:n - cp2]

        def _rope_sin_cos(seq_len, dim):
            inv_freq = 1.0 / 10000.0 ** (jnp.arange(0, dim, 2, dtype=jnp.float32) / dim)
            freqs = jnp.outer(jnp.arange(seq_len, dtype=jnp.float32), inv_freq)
            sin = jnp.concatenate([jnp.sin(freqs), jnp.sin(freqs)], axis=-1)
            cos = jnp.concatenate([jnp.cos(freqs), jnp.cos(freqs)], axis=-1)
            return (sin, cos)

        def _rotate_half(x):
            x1, x2 = jnp.split(x, 2, axis=-1)
            return jnp.concatenate([-x2, x1], axis=-1)
        b, s, dm = x.shape
        h, f = (w_qkv.shape[1], w_qkv.shape[2])
        dh = f // 3
        qkv = jnp.einsum('bsd,dhf->bshf', x, w_qkv) + b_qkv
        q, k, v = jnp.split(qkv, 3, axis=-1)
        sin, cos = _rope_sin_cos(s, dh)
        sin, cos = (sin[:, None, :], cos[:, None, :])
        q = q * cos + _rotate_half(q) * sin
        k = k * cos + _rotate_half(k) * sin
        q = q.transpose(0, 2, 1, 3)
        k = k.transpose(0, 2, 1, 3)
        v = v.transpose(0, 2, 1, 3)
        scores = jnp.einsum('bhqd,bhkd->bhqk', q, k) / jnp.sqrt(jnp.float32(f))
        slopes = jnp.asarray(_get_slopes(h), dtype=jnp.float32)
        pos = jnp.arange(s, dtype=jnp.float32)
        rel = pos[None, :] - pos[:, None]
        rel = jnp.where(rel > 0, 0.0, rel)
        alibi = rel[None, :, :] * slopes[:, None, None] * MAX_BIAS
        scores = scores + alibi[None]
        causal = jnp.tril(jnp.ones((s, s), dtype=jnp.float32))
        scores = jnp.where(causal == 0, -1000000000.0, scores)
        weights = jax.nn.softmax(scores, axis=-1)
        attn = jnp.einsum('bhqk,bhkd->bhqd', weights, v).transpose(0, 2, 1, 3)
        return jnp.einsum('bshd,hdm->bsm', attn, w_out) + b_out

    def _L0_ffn_ref(x, Wg, bg, W1, b1, W2, b2):
        import jax, jax.numpy as jnp
        import numpy as np
        B, S, D, H, E = (4, 256, 128, 512, 8)
        THRESHOLD = 0.5
        b, s, d = x.shape
        x_flat = x.reshape(-1, d)
        probs = jax.nn.sigmoid(x_flat @ Wg + bg)
        mask = (probs > THRESHOLD).astype(x_flat.dtype)
        weights = probs * mask
        h = jax.nn.relu(jnp.einsum('td,edh->eth', x_flat, W1) + b1[:, None, :])
        expert_out = jnp.einsum('eth,ehd->etd', h, W2) + b2[:, None, :]
        combined = jnp.einsum('te,etd->td', weights, expert_out)
        return combined.reshape(b, s, d)
    x = L0_attn_x
    mod = (_silu(L0_c) @ L0_wmod).reshape(L0_c.shape[0], 6, 1, -1)
    sa, ca, ga, sb, cb, gb = (mod[:, 0], mod[:, 1], mod[:, 2], mod[:, 3], mod[:, 4], mod[:, 5])
    ga = (2 * (ga >= 0) - 1) * jnp.maximum(jnp.abs(ga), 0.25)
    gb = (2 * (gb >= 0) - 1) * jnp.maximum(jnp.abs(gb), 0.25)
    h = _layernorm(x, axis=-1) * (1 + ca) + sa
    x = x + ga * _L0_attn_ref(h, L0_attn_w_qkv, L0_attn_b_qkv, L0_attn_w_out, L0_attn_b_out)
    h = _layernorm(x, axis=-1) * (1 + cb) + sb
    x = x + gb * _L0_ffn_ref(h, L0_ffn_Wg, L0_ffn_bg, L0_ffn_W1, L0_ffn_b1, L0_ffn_W2, L0_ffn_b2)
    return x

_drawn_inputs = setup_inputs


def setup_inputs(seed=0):
    import zlib

    import numpy as np

    out = dict(_drawn_inputs(seed))
    spreads = {'L0_attn_b_qkv': (0.0, 0.303), 'L0_attn_b_out': (0.0, 0.328)}
    factors = {'L0_ffn_bg': 4.637, 'L0_ffn_b1': 8.0, 'L0_ffn_b2': 7.133}
    for name, (base, spread) in spreads.items():
        noise = np.random.default_rng([zlib.crc32(name.encode()), seed]).standard_normal(out[name].shape)
        drawn = base * np.exp(spread * noise) if base else spread * noise
        out[name] = jnp.asarray(drawn.astype(out[name].dtype))
    for name, factor in factors.items():
        out[name] = (out[name] * factor).astype(out[name].dtype)
    return out
```

```python
from contextlib import ExitStack

import concourse.bass as bass
from concourse import mybir

F32 = mybir.dt.float32
F32R = mybir.dt.float32r
BF16 = mybir.dt.bfloat16
ALU = mybir.AluOpType
ACT = mybir.ActivationFunctionType
AX = mybir.AxisListType

P = 128
T = 2048
D = 128
H = 16
DH = 64
NT = T // P
TB = 512
NB = T // TB
TPB = TB // P
E = 8
HID = 512
HC = HID // P
EPS = 1e-5
QKW = 256
NEXT = 4
KA = DH + NEXT
KM = KA + 1
VW = DH + 1
NP = 4
CREDIT = 64

STEPS = []
for _b in range(NB):
    for _kt in range(TPB * (_b + 1)):
        _d = max(0, _kt - TPB * _b)
        STEPS.append((_b, _kt, TB * _b + P * _d, TB - P * _d))
NS = len(STEPS)
BLOCK_END = [max(n for n, s in enumerate(STEPS) if s[0] == b) + 1 for b in range(NB)]
CHUNKS = []
for _qt in range(NT):
    for _k0 in range(0, P * (_qt + 1), TB):
        _n = min(TB, P * (_qt + 1) - _k0)
        CHUNKS.append((_qt, _k0, _n, _k0 + _n == P * (_qt + 1)))
NC = len(CHUNKS)

PROJ_AT = [4, 6, 7, 9]
MAX_FROM, MAX_TO = 10, 34
FINAL_AT = MAX_TO
CHUNKS_AT = [[] for _ in range(NS)]
for _c in range(NC):
    CHUNKS_AT[MAX_FROM + _c * (MAX_TO - MAX_FROM) // NC].append(_c)


class Head:

    def __init__(self, pair, par):
        self.pair, self.par = pair, par

    def plus(self, n):
        k = self.par + n
        return Head(self.pair + k // 2, k % 2)

    def count(self, per, k):
        return self.pair * (2 * per) + (self.par * per + k + CREDIT)

    def turns(self, per):
        return self.pair * per + (per + CREDIT)


def wait(engine, semaphore, value):
    if not isinstance(value, int) or value > CREDIT:
        engine.wait_ge(semaphore, value)


def build(nc, x, c_col, wmod, cossin, ext, ext_scale, consts, wqk, bqk, wv, bv, wout, bout,
          wg, bg, w1, b1, w2, b2, out):
    ctx = ExitStack()
    with ctx:
        def sb(name, shape, dt):
            return ctx.enter_context(nc.sbuf_tensor(name, shape, dt))

        def ps(name):
            return ctx.enter_context(nc.psum_tensor(name, [P, 2, TB], F32))

        def sem(name):
            return ctx.enter_context(nc.semaphore(name))

        v_dram = nc.dram_tensor("v_scratch", [H, P, NT, DH], F32).ap()
        att_dram = nc.dram_tensor("att_scratch", [T, H * DH], F32).ap()
        wt_dram = nc.dram_tensor("router_scratch", [E, T], F32).ap()

        psS, psM, psV, psJ = ps("psS"), ps("psM"), ps("psV"), ps("psJ")

        xt = sb("xt", [P, NT, D], F32)
        hTh = sb("hTh", [P, T], F32R)
        hTl = sb("hTl", [P, T], F32R)
        Kx = sb("Kx", [P, 2, T], F32R)
        Qx = sb("Qx", [P, 2, T], F32R)
        Kl = sb("Kl", [P, 2, T], F32R)
        Ql = sb("Ql", [P, 2, T], F32R)
        qk_hi = sb("qk_hi", [P, T], F32R)
        qk_lo = sb("qk_lo", [P, T], F32R)
        qk = sb("qk", [P, T], F32)
        rope_sin = sb("rope_sin", [P, 2, TB], F32)
        prob = sb("prob", [P, NP, TB], F32)
        cs = sb("cs", [P, 2, T], F32)
        extb = sb("extb", [P, T], F32)
        exts = sb("exts", [P, H], F32)
        wf = sb("wf", [P, 2, QKW], F32)
        wh = sb("wh", [P, 2, QKW], F32R)
        wl = sb("wl", [P, 2, QKW], F32R)
        bqk_sb = sb("bqk_sb", [P, 2, H], F32)
        vh = sb("vh", [P, 2, NT, VW], F32)
        att = sb("att", [P, 2, NT, DH], F32)
        stage = sb("stage", [P, E * HC * D], F32)
        cst = sb("cst", [P, 3, P], F32)
        eye16 = sb("eye16", [P, P], BF16)
        maskq = sb("maskq", [P, P], BF16)
        maskk = sb("maskk", [P, P], BF16)
        ones = sb("ones", [P, P], F32)
        mxp = sb("mxp", [P, NT, NB], F32)
        mx = sb("mx", [P, NT], F32)
        negm = sb("negm", [NT, P], F32R)
        rden = sb("rden", [P, TPB], F32)
        ccol = sb("ccol", [P, 4], F32)
        modc = sb("modc", [P, 8], F32)
        ga = sb("ga", [P, D], F32)
        gtmp = sb("gtmp", [P, 2, D], F32)
        stats = sb("stats", [P, NT, 6], F32)
        mv = sb("mv", [P, NT, 2], F32)
        rstd = sb("rstd", [P, NT], F32)
        brow = sb("brow", [1, 2, D], F32)
        bvc = sb("bvc", [P, 8], F32)
        wg_sb = sb("wg_sb", [P, E], F32)
        bg_sb = sb("bg_sb", [E, 2], F32)
        b1_sb = sb("b1_sb", [P, E * HC], F32)
        b2_sb = sb("b2_sb", [E, D], F32)
        xn2 = sb("xn2", [P, 2, D], F32)
        x2 = sb("x2", [P, 2, D], F32)
        wo_f = sb("wo_f", [P, 8 * D], F32)
        wo_hi = sb("wo_hi", [P, 8 * D], F32R)
        wo_lo = sb("wo_lo", [P, 8 * D], F32R)

        eye = cst[:, 0, :]
        w_mod = prob[:, 0:2, :].rearrange("p a b -> p (a b)")[:, 0:6 * D]
        wv_f = att[:, 0, :, :].rearrange("p a b -> p (a b)")
        k1h, k1l = (a[:].rearrange("p a b -> p (a b)") for a in (Kx, Qx))
        k2h, k2l = (a[:].rearrange("p a b -> p (a b)") for a in (Kl, Ql))
        w1_f = cs[:].rearrange("p a b -> p (a b)")
        w2_f = stage[:]
        router = qk[0:E, :]
        h2 = extb[:]
        spread = [stage[:], cs[:].rearrange("p a b -> p (a b)")]
        acc, ctmp = rope_sin[:, 0, :], rope_sin[:, 1, :]
        gacc = att[:, 0, :, :].rearrange("p a b -> p (a b)")[:, 0:TB]

        s_ld = sem("setup_loaded")
        s_ld_tab = sem("tables_loaded")
        s_ld_w1 = sem("expert_weights_1_loaded")
        s_v0 = sem("vector_setup_step")
        s_a0 = sem("scalar_setup_step")
        s_p0 = sem("tensor_setup_step")
        s_vproj = sem("value_tile_projected")
        s_vcopy_a = sem("value_tile_copied_by_scalar")
        s_vcopy_v = sem("value_tile_copied_by_vector")
        s_vst = [sem("value_tile_stored_0"), sem("value_tile_stored_1")]
        s_w = [sem("qk_weights_loaded_0"), sem("qk_weights_loaded_1")]
        s_v = [sem("values_loaded_0"), sem("values_loaded_1")]
        s_kq = [sem("score_operands_placed_0"), sem("score_operands_placed_1")]
        s_mrow = [sem("max_row_placed_0"), sem("max_row_placed_1")]
        s_att_st = [sem("attention_stored_0"), sem("attention_stored_1")]
        s_wh = sem("qk_weights_high")
        s_wl = sem("qk_weights_low")
        s_proj = sem("block_projected")
        s_rope = sem("rope_terms")
        s_qk = sem("rope_sum")
        s_hi = sem("qk_high_part")
        s_lo = sem("qk_low_part")
        s_ext = sem("alibi_rows")
        s_mm = sem("max_chunk_scored")
        s_red = sem("max_chunk_reduced")
        s_m = sem("row_maxima")
        s_mt = sem("row_maxima_turned")
        s_neg = sem("row_maxima_negated")
        s_sc = sem("step_scored")
        s_exp = sem("step_exponentiated")
        s_pv = sem("step_weighted")
        s_rden = sem("row_sums_inverted")
        s_att = sem("block_normalised")
        looped = [*s_w, *s_v, *s_kq, *s_mrow, *s_att_st, s_wh, s_wl, s_proj, s_rope, s_qk, s_hi, s_lo, s_ext, s_mm, s_red, s_m, s_mt,
                  s_neg, s_sc, s_exp, s_pv, s_rden, s_att]
        s_at = [sem("attention_tile_loaded_0"), sem("attention_tile_loaded_1")]
        s_atT = sem("attention_tile_turned")
        s_ah = sem("attention_tile_high")
        s_al = sem("attention_tile_low")
        s_y = sem("tile_projected")
        s_x2 = sem("second_norm_step")
        s_xT = sem("normalised_tile_turned")
        s_sq = sem("tile_deviation")
        s_h2 = sem("modulated_tile")
        s_h2h = sem("modulated_block_high")
        s_h2l = sem("modulated_block_low")
        looped += [*s_at, s_atT, s_ah, s_al, s_y, s_x2, s_sq, s_xT, s_h2]
        s_z = sem("router_scored")
        s_ez = sem("router_exp")
        s_r = sem("router_step")
        s_wt_st = sem("router_weights_stored")
        s_wb = [sem("router_weights_spread_0"), sem("router_weights_spread_1")]
        s_fw = sem("expert_weights_split")
        s_fwh = sem("expert_weights_high")
        s_u = sem("hidden_scored")
        s_hf = sem("hidden_relu")
        s_hh = sem("hidden_high")
        s_hl = sem("hidden_low")
        s_dn = sem("hidden_consumed")
        s_o = sem("expert_biases")
        s_c = sem("expert_combined")
        s_yt = sem("output_turned")
        s_out = sem("output_tile")
        s_st = sem("output_stored")
        looped += [*s_wb, s_dn, s_u, s_hf, s_hh, s_hl, s_o, s_c, s_yt, s_out]

        block = ctx.enter_context(nc.Block())
        mark = {}
        ALL = {name: count * H + CREDIT for name, count in
               (("sc", NS), ("exp", NS), ("lo", NB), ("hi", NB), ("rope", 2 * NB), ("att", NB), ("neg", 1), ("pv", NS))}

        def slots(engine, slot):
            slot(Head(-1, 0), False, False, True)
            slot(Head(-1, 1), False, True, True)
            with engine.Fori(0, H // 2 - 1) as pair:
                slot(Head(pair, 0), True, True, True)
                slot(Head(pair, 1), True, True, True)
            slot(Head(H // 2 - 1, 0), True, True, False)
            slot(Head(H // 2 - 1, 1), True, False, False)

        def tiles(engine, step):
            step(Head(0, 0), True, False, False)
            step(Head(0, 1), True, True, False)
            with engine.Fori(1, NT // 2) as pair:
                step(Head(pair, 0), True, True, True)
                step(Head(pair, 1), True, True, True)
            step(Head(NT // 2, 0), False, True, True)
            step(Head(NT // 2, 1), False, False, True)

        def index(h):
            return h.pair * 2 + h.par

        def hidden(buf, i):
            return buf[:, (i % 4) * TB:(i % 4 + 1) * TB]

        setup_loads = [
            (xt[:], x.rearrange("(n p) d -> p n d", p=P)), (ccol[:, 0:1], c_col), (w_mod, wmod),
            (cst[:], consts), (wv_f, wv), (wo_f[:], wout), (bvc[:], bv), (brow[:, 0, :], bout),
            (bqk_sb[:], bqk), (wg_sb[:], wg), (bg_sb[:, 0:1], bg), (b1_sb[:], b1), (b2_sb[:], b2)]
        table_loads = [
            (cs[:], cossin), (extb[64:68, :], ext[0]), (extb[96:100, :], ext[1]),
            (exts[64:68, :], ext_scale[0]), (exts[96:100, :], ext_scale[1]), (w2_f, w2)]

        @block.vector
        def _(dve):
            n = [0]

            def link(ins, name=None):
                n[0] += 1
                ins.then_inc(s_v0, 1)
                dve.wait_ge(s_v0, n[0])
                if name:
                    mark[name] = n[0]

            link(dve.memset(ones[:], 1.0))
            link(dve.memset(mxp[:], -3.0e38))
            link(dve.memset(vh[:], 1.0))
            for par in range(2):
                link(dve.memset(Kx[64:96, par, :].bitcast(F32), 1.0), "ones")
            dve.wait_ge(s_ld, 16 * len(setup_loads))
            link(dve.tensor_copy(eye16[:], cst[:, 0, :]))
            link(dve.tensor_copy(maskq[:], cst[:, 1, :]))
            link(dve.tensor_copy(maskk[:], cst[:, 2, :]))
            dve.wait_ge(s_a0, 1)
            link(dve.tensor_scalar(ccol[:, 2:3], ccol[:, 1:2], 1.0, None, ALU.add))
            link(dve.reciprocal(ccol[:, 3:4], ccol[:, 2:3]))
            link(dve.tensor_tensor(ccol[:, 1:2], ccol[:, 0:1], ccol[:, 3:4], ALU.mult))
            link(dve.tensor_scalar(gtmp[:, 0, :], ones[:], ccol[:, 1:2], None, ALU.mult), "silu")
            for t in range(NT):
                dve.bn_stats(stats[:, t, :], xt[:, t, :]).then_inc(s_v0, 1)
            n[0] += NT
            dve.wait_ge(s_v0, n[0])
            for t in range(NT):
                dve.bn_aggr(mv[:, t, :], stats[:, t, :]).then_inc(s_v0, 1)
            n[0] += NT
            dve.wait_ge(s_v0, n[0])
            link(dve.tensor_scalar(rstd[:], mv[:, :, 1], EPS, None, ALU.add), "var")
            dve.wait_ge(s_a0, 2)
            link(dve.reciprocal(rstd[:], rstd[:]))
            for t in range(NT):
                dve.tensor_scalar(qk[:, t * D:(t + 1) * D], xt[:, t, :], mv[:, t, 0:1], rstd[:, t:t + 1],
                                  ALU.subtract, ALU.mult).then_inc(s_v0, 1)
                n[0] += 1
                mark["xn", t] = n[0]
            dve.wait_ge(s_p0, 1)
            link(dve.tensor_copy(modc[:, 0:6], psJ[:, 0, 0:6]))
            link(dve.tensor_scalar(modc[:, 1:2], modc[:, 1:2], 1.0, None, ALU.add))
            link(dve.tensor_scalar(modc[:, 4:5], modc[:, 4:5], 1.0, None, ALU.add))
            link(dve.tensor_copy(ga[:], psJ[:, 1, 0:D]), "mod")
            for g, sg, mg in ((ga[:], gtmp[:, 0, :], gtmp[:, 1, :]),
                              (modc[:, 5:6], ccol[:, 2:3], ccol[:, 3:4])):
                link(dve.tensor_scalar(sg, g, 0.0, 2.0, ALU.is_ge, ALU.mult))
                link(dve.tensor_scalar(sg, sg, -1.0, None, ALU.add))
                link(dve.tensor_tensor(mg, g, sg, ALU.mult))
                link(dve.scalar_tensor_tensor(g, mg, 0.25, sg, ALU.max, ALU.mult))
            link(dve.tensor_scalar(bg_sb[:, 1:2], bg_sb[:, 0:1], -1.0, None, ALU.mult), "bg")
            for b in range(NB):
                dve.wait_ge(s_p0, 2 + b)
                if b >= 2:
                    dve.wait_ge(s_a0, b + 1)
                link(dve.tensor_scalar(rope_sin[:, b % 2, :], psS[:, b % 2, :], modc[:, 1:2], modc[:, 0:1],
                                       ALU.mult, ALU.add), ("hT", b))
                dve.wait_ge(s_a0, 3 + b)
                link(dve.tensor_tensor(hTl[:, b * TB:(b + 1) * TB], rope_sin[:, b % 2, :],
                                       hTh[:, b * TB:(b + 1) * TB], ALU.subtract), ("hTl", b))
            dve.wait_ge(s_a0, 7)
            link(dve.tensor_tensor(qk_lo[:, 0:H * DH], wv_f, qk_hi[:, 0:H * DH], ALU.subtract), "wvl")
            dve.wait_ge(s_a0, 8)
            link(dve.tensor_tensor(wo_lo[:], wo_f[:], wo_hi[:], ALU.subtract), "wol")
            for t in range(NT):
                dve.wait_ge(s_vproj, t + 1)
                if t >= 2:
                    dve.wait_ge(s_vst[t % 2], 16 * (t // 2))
                dve.tensor_copy(prob[:, 2 * (t % 2) + 1, :],
                                (psV if t % 2 else psM)[:, 1, :]).then_inc(s_vcopy_v, 1)
            dve.wait_ge(s_p0, 6)
            link(dve.tensor_tensor(brow[:, 1, :], psJ[0:1, 0, 0:D], brow[:, 0, :], ALU.add), "brow")
            dve.wait_ge(s_ld_tab, 16 * len(table_loads))

            def rope(g, b):
                t = slice(b * TB, (b + 1) * TB)
                wait(dve, s_proj, g.count(NB, b + 1))
                wait(dve, s_lo, g.count(NB, b + 1 - NB))
                dve.scalar_tensor_tensor(qk[:, t], psJ[:, 0, :], bqk_sb[:, 0, bass.ds(index(g), 1)],
                                         cs[:, 0, t], ALU.add, ALU.mult).then_inc(s_rope, 1)
                wait(dve, s_qk, g.count(NB, b - 1))
                dve.scalar_tensor_tensor(rope_sin[:, b % 2, :], psJ[:, 1, :],
                                         bqk_sb[:, 1, bass.ds(index(g), 1)], cs[:, 1, t],
                                         ALU.add, ALU.mult).then_inc(s_rope, 1)

            def alibi(g):
                wait(dve, s_sc, g.count(NS, -NS))
                wait(dve, s_lo, g.count(NB, NB))
                dve.tensor_scalar(Kx[64:68, g.par, :], extb[64:68, :], exts[64:68, bass.ds(index(g), 1)], None,
                                  ALU.mult).then_inc(s_ext, 1)
                dve.tensor_scalar(Qx[64:68, g.par, :], extb[96:100, :], exts[96:100, bass.ds(index(g), 1)],
                                  None, ALU.mult).then_inc(s_ext, 1)

            def reduce_chunk(g, c):
                qt, k0, w, _ = CHUNKS[c]
                wait(dve, s_mm, g.count(NC, c + 1))
                if c == 0:
                    wait(dve, s_m, g.count(1, 0))
                dve.tensor_reduce(mxp[:, qt, k0 // TB:k0 // TB + 1], psM[:, c % 2, 0:w], AX.X,
                                  ALU.max).then_inc(s_red, 1)

            def maxima(g):
                wait(dve, s_red, g.count(NC, NC))
                dve.tensor_reduce(mx[:], mxp[:], AX.X, ALU.max).then_inc(s_m, 1)
                wait(dve, s_mt, g.count(1, 1))
                wait(dve, s_mrow[g.plus(-1).par], g.plus(-1).turns(16))
                dve.tensor_scalar(negm[:], psM[0:NT, 0, 0:P], -1.0, None, ALU.mult).then_inc(s_neg, 1)

            def normalise(h, b):
                wait(dve, s_pv, h.count(NS, BLOCK_END[b]))
                wait(dve, s_att, h.count(NB, b))
                vals = psV[:, b % 2, 0:TPB * VW].rearrange("p (t w) -> p t w", w=VW)
                dve.reciprocal(rden[:], vals[:, :, DH]).then_inc(s_rden, 1)
                wait(dve, s_rden, h.count(NB, b + 1))
                if b == 0:
                    wait(dve, s_att_st[h.par], h.plus(-2).turns(16))
                dve.tensor_tensor(att[:, h.par, b * TPB:(b + 1) * TPB, :], vals[:, :, 0:DH],
                                  rden[:].unsqueeze(2).to_broadcast([P, TPB, DH]),
                                  ALU.mult).then_inc(s_att, 1)

            def slot(h, attend, maximum, project):
                for j in range(NS):
                    if attend and j in BLOCK_END:
                        normalise(h, BLOCK_END.index(j))
                    if project and j in PROJ_AT:
                        rope(h.plus(2), PROJ_AT.index(j))
                    if maximum:
                        for c in CHUNKS_AT[j]:
                            reduce_chunk(h.plus(1), c)
                        if j == FINAL_AT:
                            maxima(h.plus(1))
                if project:
                    alibi(h.plus(2))
                if attend:
                    normalise(h, NB - 1)

            slots(dve, slot)

            def low_tile(t):
                k = t.par
                wait(dve, s_ah, t.count(1, 1))
                wait(dve, s_y, t.count(1, -1))
                dve.tensor_tensor(qk_lo[:, k * 1024:(k + 1) * 1024],
                                  (psM if k else psS)[:].rearrange("p a b -> p (a b)"),
                                  qk_hi[:, k * 1024:(k + 1) * 1024], ALU.subtract).then_inc(s_al, 1)

            def norm_tile(t):
                k = t.par
                step = [0]

                def then(ins, needed=True):
                    step[0] += 1
                    ins.then_inc(s_x2, 1)
                    if needed:
                        wait(dve, s_x2, t.count(8, step[0]))

                wait(dve, s_y, t.count(1, 1))
                xcur = xt[:, bass.ds(index(t), 1), :].rearrange("p a b -> p (a b)")
                then(dve.tensor_tensor(gtmp[:, k, :], psV[:, k, 0:D], ga[:], ALU.mult))
                then(dve.tensor_tensor(x2[:, k, :], gtmp[:, k, :], xcur, ALU.add))
                then(dve.bn_stats(stats[:, k, :], x2[:, k, :]))
                then(dve.tensor_scalar(xcur, x2[:, k, :], 1.0, None, ALU.mult), False)
                then(dve.bn_aggr(mv[:, k, :], stats[:, k, :]))
                then(dve.tensor_scalar(rstd[:, k:k + 1], mv[:, k, 1:2], EPS, None, ALU.add))
                wait(dve, s_sq, t.count(1, 1))
                then(dve.reciprocal(rstd[:, k:k + 1], rstd[:, k:k + 1]))
                wait(dve, s_xT, t.count(1, -1))
                dve.tensor_scalar(xn2[:, k, :], x2[:, k, :], mv[:, k, 0:1], rstd[:, k:k + 1],
                                  ALU.subtract, ALU.mult).then_inc(s_x2, 1)

            def modulate_tile(t):
                wait(dve, s_xT, t.count(1, 1))
                dve.tensor_scalar(extb[:, bass.ds(index(t) * P, P)], psJ[:, t.par, 0:P], modc[:, 4:5],
                                  modc[:, 3:4], ALU.mult, ALU.add).then_inc(s_h2, 1)

            def tile_step(t, turn, project, modulate):
                if turn:
                    low_tile(t)
                if project:
                    norm_tile(t.plus(-1))
                if modulate:
                    modulate_tile(t.plus(-2))

            tiles(dve, tile_step)

            for b in range(NB):
                t = slice(b * TB, (b + 1) * TB)
                dve.wait_ge(s_ez, b + 1)
                dve.tensor_scalar(router[:, t], router[:, t], 1.0, None, ALU.add).then_inc(s_r, 1)
                dve.wait_ge(s_r, 3 * b + 1)
                dve.reciprocal(router[:, t], router[:, t]).then_inc(s_r, 1)
                dve.wait_ge(s_r, 3 * b + 2)
                dve.scalar_tensor_tensor(router[:, t], router[:, t], 0.5, router[:, t], ALU.is_gt,
                                         ALU.mult).then_inc(s_r, 1)

            def hidden_low(tb, i):
                wait(dve, s_hf, tb.count(E * HC, i + 1))
                wait(dve, s_hh, tb.count(E * HC, i + 1))
                wait(dve, s_dn, tb.count(E * HC, i - 3))
                dve.tensor_tensor(hidden(qk_lo, i), prob[:, i % 4, :], hidden(qk_hi, i),
                                  ALU.subtract).then_inc(s_hl, 1)

            def combine(tb, e):
                wait(dve, s_dn, tb.count(E * HC, HC * (e + 1)))
                wait(dve, s_c, tb.count(2 * E + 2, 2 * e + 1))
                dve.tensor_tensor(ctmp, psV[:, (e + 1) % 2, :], spread[tb.par][:, e * TB:(e + 1) * TB],
                                  ALU.mult).then_inc(s_c, 1)
                wait(dve, s_c, tb.count(2 * E + 2, 2 * e + 2))
                dve.tensor_tensor(acc, acc, ctmp, ALU.add).then_inc(s_c, 1)

            with dve.Fori(0, NB // 2) as pair:
                for k in range(2):
                    tb = Head(pair, k)
                    wait(dve, s_o, tb.count(1, 1))
                    wait(dve, s_c, tb.count(2 * E + 2, 0))
                    dve.tensor_copy(acc, psV[:, 0, :]).then_inc(s_c, 1)
                    for i in range(E * HC):
                        hidden_low(tb, i)
                        if i == 6:
                            wait(dve, s_wb[k], tb.turns(16))
                        if i >= 6 and (i - 6) % HC == 0:
                            combine(tb, (i - 6) // HC)
                    combine(tb, E - 1)
                    wait(dve, s_c, tb.count(2 * E + 2, 2 * E + 1))
                    wait(dve, s_yt, tb.count(1, 0))
                    dve.tensor_scalar(gacc, acc, modc[:, 5:6], None, ALU.mult).then_inc(s_c, 1)
                    wait(dve, s_yt, tb.count(1, 1))
                    xb = xt[:, bass.ds(index(tb) * TPB, TPB), :].rearrange("p a b -> p (a b)")
                    dve.tensor_tensor(xb, psJ[:, k, :], xb, ALU.add).then_inc(s_out, 1)

        @block.scalar
        def _(act):
            act.wait_ge(s_ld, 16 * len(setup_loads))
            act.activation(ccol[:, 1:2], ccol[:, 0:1], ACT.Exp, scale=-1.0).then_inc(s_a0, 1)
            act.wait_ge(s_v0, mark["var"])
            act.activation(rstd[:], rstd[:], ACT.Sqrt).then_inc(s_a0, 1)
            for b in range(NB):
                act.wait_ge(s_v0, mark["hT", b])
                act.copy(hTh[:, b * TB:(b + 1) * TB], rope_sin[:, b % 2, :]).then_inc(s_a0, 1)
            act.copy(qk_hi[:, 0:H * DH], wv_f).then_inc(s_a0, 1)
            act.copy(wo_hi[:], wo_f[:]).then_inc(s_a0, 1)
            for t in range(NT):
                act.wait_ge(s_vproj, t + 1)
                if t >= 2:
                    act.wait_ge(s_vst[t % 2], 16 * (t // 2))
                act.copy(prob[:, 2 * (t % 2), :], (psV if t % 2 else psM)[:, 0, :]).then_inc(s_vcopy_a, 1)
            for par in range(2):
                act.wait_ge(s_vst[par], 16 * NT // 2)

            def weights_high(g):
                wait(act, s_w[g.par], g.turns(16))
                wait(act, s_proj, g.count(NB, -NB))
                act.copy(wh[:, g.par, :], wf[:, g.par, :]).then_inc(s_wh, 1)

            def high(g, b):
                t = slice(b * TB, (b + 1) * TB)
                wait(act, s_qk, g.count(NB, b + 1))
                if b == 0:
                    wait(act, s_kq[g.plus(-1).par], g.plus(-1).turns(96))
                act.copy(qk_hi[:, t], qk[:, t]).then_inc(s_hi, 1)

            def exponentiate(h, j):
                w = STEPS[j][3]
                wait(act, s_sc, h.count(NS, j + 1))
                wait(act, s_pv, h.count(NS, j + 1 - NP))
                act.activation(prob[:, j % NP, 0:w], psS[:, j % 2, 0:w], ACT.Exp).then_inc(s_exp, 1)

            def slot(h, attend, maximum, project):
                if project:
                    weights_high(h.plus(2))
                for j in range(NS):
                    if attend:
                        exponentiate(h, j)
                    if project and j - 2 in PROJ_AT:
                        high(h.plus(2), PROJ_AT.index(j - 2))

            slots(act, slot)

            act.wait_ge(s_sc, ALL["sc"])
            act.wait_ge(s_ld_w1, 16)
            act.copy(k1h, w1_f).then_inc(s_fwh, 1)
            act.copy(k2h, w2_f).then_inc(s_fwh, 1)

            def tile_step(t, turn, project, modulate):
                if turn:
                    k = t.par
                    wait(act, s_atT, t.count(1, 1))
                    wait(act, s_y, t.count(1, -1))
                    act.copy(qk_hi[:, k * 1024:(k + 1) * 1024],
                             (psM if k else psS)[:].rearrange("p a b -> p (a b)")).then_inc(s_ah, 1)
                if project:
                    n = t.plus(-1)
                    wait(act, s_x2, n.count(8, 6))
                    act.activation(rstd[:, n.par:n.par + 1], rstd[:, n.par:n.par + 1],
                                   ACT.Sqrt).then_inc(s_sq, 1)

            tiles(act, tile_step)

            act.wait_ge(s_h2, NT + CREDIT)
            for b in range(NB):
                act.copy(hTh[:, b * TB:(b + 1) * TB], h2[:, b * TB:(b + 1) * TB]).then_inc(s_h2h, 1)
                act.wait_ge(s_z, b + 1)
                act.activation(router[:, b * TB:(b + 1) * TB], psJ[0:E, b % 2, :], ACT.Exp,
                               bias=bg_sb[:, 1:2], scale=-1.0).then_inc(s_ez, 1)

            with act.Fori(0, NB // 2) as pair:
                for k in range(2):
                    tb = Head(pair, k)
                    for i in range(E * HC):
                        u = (psS, psM)[i % 4 // 2][:, i % 2, :]
                        wait(act, s_u, tb.count(E * HC, i + 1))
                        wait(act, s_hl, tb.count(E * HC, i - 3))
                        act.activation(prob[:, i % 4, :], u, ACT.Relu,
                                       bias=b1_sb[:, i:i + 1]).then_inc(s_hf, 1)
                        wait(act, s_dn, tb.count(E * HC, i - 3))
                        act.activation(hidden(qk_hi, i), u, ACT.Relu,
                                       bias=b1_sb[:, i:i + 1]).then_inc(s_hh, 1)

        @block.gpsimd
        def _(pool):
            pool.wait_ge(s_vproj, NT)

            def weights_low(g):
                wait(pool, s_wh, g.count(1, 1))
                wait(pool, s_w[g.par], g.turns(16))
                wait(pool, s_proj, g.count(NB, -NB))
                pool.tensor_tensor(wl[:, g.par, :], wf[:, g.par, :], wh[:, g.par, :],
                                   ALU.subtract).then_inc(s_wl, 1)

            def sum_block(g, b):
                t = slice(b * TB, (b + 1) * TB)
                wait(pool, s_rope, g.count(2 * NB, 2 * b + 2))
                pool.tensor_tensor(qk[:, t], qk[:, t], rope_sin[:, b % 2, :], ALU.add).then_inc(s_qk, 1)

            def low_block(g, b):
                t = slice(b * TB, (b + 1) * TB)
                wait(pool, s_hi, g.count(NB, b + 1))
                if b == 0:
                    wait(pool, s_kq[g.plus(-1).par], g.plus(-1).turns(96))
                pool.tensor_tensor(qk_lo[:, t], qk[:, t], qk_hi[:, t], ALU.subtract).then_inc(s_lo, 1)

            def slot(h, attend, maximum, project):
                if project:
                    weights_low(h.plus(2))
                    for b in range(NB):
                        sum_block(h.plus(2), b)
                        if b:
                            low_block(h.plus(2), b - 1)
                    low_block(h.plus(2), NB - 1)

            slots(pool, slot)

            pool.wait_ge(s_fwh, 1)
            pool.tensor_tensor(k1l, w1_f, k1h, ALU.subtract).then_inc(s_fw, 1)
            pool.wait_ge(s_fwh, 2)
            pool.tensor_tensor(k2l, w2_f, k2h, ALU.subtract).then_inc(s_fw, 1)
            for b in range(NB):
                t = slice(b * TB, (b + 1) * TB)
                pool.wait_ge(s_h2h, b + 1)
                pool.tensor_tensor(hTl[:, t], h2[:, t], hTh[:, t], ALU.subtract).then_inc(s_h2l, 1)

        @block.tensor
        def _(pe):
            pe.wait_ge(s_ld, 16 * len(setup_loads))
            pe.wait_ge(s_v0, mark["silu"])
            for k in range(6):
                pe.matmul(psJ[:, 0, k:k + 1], w_mod[:, k * D:(k + 1) * D], ccol[:, 1:2],
                          start=(k == 0), stop=True, skip_group_check=True)
            pe.matmul(psJ[:, 1, 0:D], gtmp[:, 0, :], w_mod[:, 2 * D:3 * D],
                      start=True, stop=True).then_inc(s_p0, 1)
            for b in range(NB):
                if b >= 2:
                    pe.wait_ge(s_v0, mark["hT", b - 2])
                for t in range(TPB * b, TPB * (b + 1)):
                    pe.wait_ge(s_v0, mark["xn", t])
                    mm = pe.transpose(psS[:, b % 2, (t % TPB) * P:(t % TPB + 1) * P],
                                      qk[:, t * P:(t + 1) * P], eye)
                mm.then_inc(s_p0, 1)
            pe.wait_ge(s_v0, mark["mod"])
            for c in range(8):
                mm = pe.matmul(psJ[0:1, 0, 0:D], bvc[:, c:c + 1], wo_f[:, c * D:(c + 1) * D],
                               start=(c == 0), stop=(c == 7))
            mm.then_inc(s_p0, 1)
            pe.wait_ge(s_v0, mark["wvl"])
            for t in range(NT):
                if t >= 2:
                    pe.wait_ge(s_vcopy_a, t - 1)
                    pe.wait_ge(s_vcopy_v, t - 1)
                tt = slice(t * P, (t + 1) * P)
                for c in range(2):
                    cc = slice(c * TB, (c + 1) * TB)
                    o = (psV if t % 2 else psM)[:, c, :]
                    pe.matmul(o, hTh[:, tt], qk_hi[:, cc], start=True, stop=False)
                    pe.matmul(o, hTh[:, tt], qk_lo[:, cc], start=False, stop=False)
                    mm = pe.matmul(o, hTl[:, tt], qk_hi[:, cc], start=False, stop=True)
                mm.then_inc(s_vproj, 1)
            pe.wait_ge(s_vcopy_a, NT)
            pe.wait_ge(s_vcopy_v, NT)
            pe.wait_ge(s_v0, mark["brow"])

            def project(g, b):
                t = slice(b * TB, (b + 1) * TB)
                if b == 0:
                    wait(pe, s_wh, g.count(1, 1))
                    wait(pe, s_wl, g.count(1, 1))
                wait(pe, s_rope, g.count(2 * NB, 2 * b))
                for half in range(2):
                    o, c = psJ[:, half, :], slice(half * P, (half + 1) * P)
                    pe.matmul(o, wh[:, g.par, c], hTh[:, t], start=True, stop=False)
                    pe.matmul(o, wl[:, g.par, c], hTh[:, t], start=False, stop=False)
                    mm = pe.matmul(o, wh[:, g.par, c], hTl[:, t], start=False, stop=True)
                mm.then_inc(s_proj, 1)

            def max_chunk(g, c):
                qt, k0, w, diagonal = CHUNKS[c]
                if c == 0:
                    wait(pe, s_kq[g.par], g.turns(96))
                    wait(pe, s_ext, g.count(2, 2))
                    wait(pe, s_neg, g.count(1, 0))
                wait(pe, s_red, g.count(NC, c - 1))
                mm = pe.matmul(psM[:, c % 2, 0:w], Qx[0:KA, g.par, qt * P:(qt + 1) * P],
                               Kx[0:KA, g.par, k0:k0 + w], start=True, stop=True)
                if diagonal:
                    mm = pe.matmul(psM[:, c % 2, w - P:w], eye16[:], maskq[:], start=False, stop=True,
                                   skip_group_check=True)
                mm.then_inc(s_mm, 1)

            def turn_maxima(g):
                wait(pe, s_m, g.count(1, 1))
                pe.transpose(psM[0:NT, 0, 0:P], mx[:], eye).then_inc(s_mt, 1)

            def score(h, j):
                b, kt, q0, w = STEPS[j]
                k = slice(kt * P, (kt + 1) * P)
                if j == 0:
                    wait(pe, s_mrow[h.par], h.turns(16))
                wait(pe, s_exp, h.count(NS, j - 1))
                o = psS[:, j % 2, 0:w]
                pe.matmul(o, Kx[0:KM, h.par, k], Qx[0:KM, h.par, q0:q0 + w], start=True, stop=False)
                if kt >= TPB * b:
                    pe.matmul(psS[:, j % 2, 0:P], eye16[:], maskk[:], start=False, stop=False,
                              skip_group_check=True)
                mm = pe.matmul(o, Kl[:, h.par, k], Ql[:, h.par, q0:q0 + w], start=False, stop=True)
                mm.then_inc(s_sc, 1)

            def weigh(h, j):
                b, kt, q0, w = STEPS[j]
                if j == 0:
                    wait(pe, s_v[h.par], h.turns(16))
                if kt == 0:
                    wait(pe, s_att, h.count(NB, b - 1))
                wait(pe, s_exp, h.count(NS, j + 1))
                first = (q0 - b * TB) // P
                for t in range(first, TPB):
                    mm = pe.matmul(psV[:, b % 2, t * VW:(t + 1) * VW],
                                   prob[:, j % NP, (t - first) * P:(t - first + 1) * P],
                                   vh[:, h.par, kt, :], start=(kt == 0 and t == 0),
                                   stop=(kt == TPB * b + t), skip_group_check=True)
                mm.then_inc(s_pv, 1)

            def slot(h, attend, maximum, project_):
                for j in range(NS):
                    if attend:
                        if j + 1 < NS:
                            score(h, j + 1)
                        elif maximum:
                            score(h.plus(1), 0)
                        weigh(h, j)
                    if project_ and j in PROJ_AT:
                        project(h.plus(2), PROJ_AT.index(j))
                    if maximum:
                        for c in CHUNKS_AT[j]:
                            max_chunk(h.plus(1), c)
                        if j == FINAL_AT:
                            turn_maxima(h.plus(1))
                if maximum and not attend:
                    score(h.plus(1), 0)

            slots(pe, slot)
            pe.wait_ge(s_exp, ALL["exp"])
            pe.wait_ge(s_att, ALL["att"])
            pe.wait_ge(s_neg, ALL["neg"])

            def turn_tile(t):
                k = t.par
                wait(pe, s_at[k], t.turns(16))
                wait(pe, s_al, t.count(1, -1))
                for c in range(8):
                    mm = pe.transpose((psM if k else psS)[:, c // 4, (c % 4) * P:(c % 4 + 1) * P],
                                      qk[:, k * 1024 + c * P:k * 1024 + (c + 1) * P], eye)
                mm.then_inc(s_atT, 1)

            def out_tile(t):
                k = t.par
                wait(pe, s_al, t.count(1, 1))
                wait(pe, s_x2, t.count(8, -15))
                o = psV[:, k, 0:D]
                pe.matmul(o, ones[0:1, :], brow[:, 1, :], start=True, stop=False)
                for c in range(8):
                    a = slice(k * 1024 + c * P, k * 1024 + (c + 1) * P)
                    w = slice(c * D, (c + 1) * D)
                    pe.matmul(o, qk_hi[:, a], wo_hi[:, w], start=False, stop=False)
                    pe.matmul(o, qk_hi[:, a], wo_lo[:, w], start=False, stop=False)
                    mm = pe.matmul(o, qk_lo[:, a], wo_hi[:, w], start=False, stop=(c == 7))
                mm.then_inc(s_y, 1)

            def turn_norm(t):
                wait(pe, s_x2, t.count(8, 8))
                wait(pe, s_h2, t.count(1, -1))
                pe.transpose(psJ[:, t.par, 0:P], xn2[:, t.par, :], eye).then_inc(s_xT, 1)

            def tile_step(t, turn, project_, modulate):
                if turn:
                    turn_tile(t)
                if project_:
                    out_tile(t.plus(-1))
                if modulate:
                    turn_norm(t.plus(-2))

            tiles(pe, tile_step)

            pe.wait_ge(s_h2, NT + CREDIT)
            for b in range(NB):
                if b >= 2:
                    pe.wait_ge(s_ez, b - 1)
                pe.matmul(psJ[0:E, b % 2, :], wg_sb[:], h2[:, b * TB:(b + 1) * TB],
                          start=True, stop=True).then_inc(s_z, 1)
            pe.wait_ge(s_ez, NB)
            pe.wait_ge(s_r, 3 * NB)
            pe.wait_ge(s_x2, 8 * NT + CREDIT)
            pe.wait_ge(s_fw, 2)
            pe.wait_ge(s_h2l, NB)

            def hidden_scores(tb, i):
                t = bass.ds(index(tb) * TB, TB)
                w = slice(i * P, (i + 1) * P)
                o = (psS, psM)[i % 4 // 2][:, i % 2, :]
                wait(pe, s_hh, tb.count(E * HC, i - 3))
                pe.matmul(o, k1h[:, w], hTh[:, t], start=True, stop=False)
                pe.matmul(o, k1l[:, w], hTh[:, t], start=False, stop=False)
                pe.matmul(o, k1h[:, w], hTl[:, t], start=False, stop=True).then_inc(s_u, 1)

            def expert_out(tb, i):
                e, c = i // HC, i % HC
                w = slice(i * P, (i + 1) * P)
                o = psV[:, (e + 1) % 2, :]
                if c == 0:
                    wait(pe, s_c, tb.count(2 * E + 2, -4 if e == 0 else 1 if e == 1 else 2 * e - 2))
                wait(pe, s_hl, tb.count(E * HC, i + 1))
                pe.matmul(o, k2h[:, w], hidden(qk_hi, i), start=(c == 0), stop=False)
                pe.matmul(o, k2l[:, w], hidden(qk_hi, i), start=False, stop=False)
                mm = pe.matmul(o, k2h[:, w], hidden(qk_lo, i), start=False, stop=(c == HC - 1))
                mm.then_inc(s_dn, 1)
                return mm

            with pe.Fori(0, NB // 2) as pair:
                for k in range(2):
                    tb = Head(pair, k)
                    wait(pe, s_c, tb.count(2 * E + 2, -2))
                    pe.matmul(psV[:, 0, :], b2_sb[:], router[:, bass.ds(index(tb) * TB, TB)],
                              start=True, stop=True).then_inc(s_o, 1)
                    for i in range(E * HC + 3):
                        if i < E * HC:
                            hidden_scores(tb, i)
                        if i >= 3:
                            expert_out(tb, i - 3)
                    wait(pe, s_c, tb.count(2 * E + 2, 2 * E + 2))
                    wait(pe, s_out, tb.count(1, -1))
                    for t in range(TPB):
                        mm = pe.transpose(psJ[:, k, t * P:(t + 1) * P], gacc[:, t * P:(t + 1) * P], eye)
                    mm.then_inc(s_yt, 1)

        @block.sync
        def _(sp):
            def fixed(value):
                return value if isinstance(value, int) else sp.snap(value)

            for s in looped:
                sp.sem_inc(s, CREDIT)
            for dst, src in setup_loads:
                sp.dma_start(dst, src).then_inc(s_ld, 16)
            for dst, src in table_loads:
                sp.dma_start(dst, src).then_inc(s_ld_tab, 16)
            for t in range(NT):
                sp.wait_ge(s_vcopy_a, t + 1)
                sp.wait_ge(s_vcopy_v, t + 1)
                k = t % 2
                sp.dma_start(v_dram[:, :, t, :].rearrange("h p d -> p h d"),
                             prob[:, 2 * k:2 * k + 2, :].rearrange("p a (h d) -> p (a h) d", d=DH)
                             ).then_inc(s_vst[k], 16)
            for par in range(2):
                sp.wait_ge(s_vst[par], 16 * NT // 2)
            sp.wait_ge(s_v0, mark["brow"])

            def load_weights(g):
                n = fixed(index(g))
                wait(sp, s_wl, g.count(1, -1))
                sp.dma_start(wf[:, g.par, :], wqk[bass.ds(n, 1)].rearrange("a p c -> p (a c)")
                             ).then_inc(s_w[g.par], 16)

            def load_values(g):
                n = fixed(index(g))
                wait(sp, s_pv, g.count(NS, -NS))
                sp.dma_start(vh[:, g.par, :, 0:DH], v_dram[bass.ds(n, 1)].rearrange("a p t d -> p (a t) d")
                             ).then_inc(s_v[g.par], 16)

            def place(g):
                k = g.par
                wait(sp, s_ext, g.count(2, 2))
                for dst, src in ((Kx[0:DH, k, :], qk_hi[DH:P, :]), (Qx[0:DH, k, :], qk_hi[0:DH, :]),
                                 (Kl[0:DH, k, :], qk_lo[DH:P, :]), (Kl[DH:P, k, :], qk_hi[DH:P, :]),
                                 (Ql[0:DH, k, :], qk_hi[0:DH, :]), (Ql[DH:P, k, :], qk_lo[0:DH, :])):
                    sp.dma_start(dst.bitcast(F32), src.bitcast(F32)).then_inc(s_kq[k], 16)

            def slot(h, attend, maximum, project):
                if project:
                    load_weights(h.plus(2))
                if maximum:
                    load_values(h.plus(1))
                    g = h.plus(1)
                    wait(sp, s_neg, g.count(1, 1))
                    sp.dma_start(Qx[KA:KM, g.par, :].bitcast(F32), negm[:].bitcast(F32)).then_inc(s_mrow[g.par], 16)
                if project:
                    place(h.plus(2))
                if attend:
                    n = fixed(index(h) * DH)
                    wait(sp, s_att, h.count(NB, NB))
                    sp.dma_start(att_dram.rearrange("(n p) c -> p n c", p=P)[:, :, bass.ds(n, DH)],
                                 att[:, h.par, :, :]).then_inc(s_att_st[h.par], 16)

            slots(sp, slot)
            sp.wait_ge(s_rope, ALL["rope"])
            sp.dma_start(w1_f, w1).then_inc(s_ld_w1, 16)
            for par in range(2):
                sp.wait_ge(s_att_st[par], 16 * H // 2 + CREDIT)
            sp.wait_ge(s_lo, ALL["lo"])

            with sp.Fori(0, NT // 2) as pair:
                for k in range(2):
                    t = Head(pair, k)
                    n = fixed(index(t) * P)
                    wait(sp, s_atT, t.count(1, -1))
                    sp.dma_start(qk[:, k * 1024:(k + 1) * 1024],
                                 att_dram[bass.ds(n, P), :]).then_inc(s_at[k], 16)

            sp.wait_ge(s_r, 3 * NB)
            sp.dma_start(wt_dram, router).then_inc(s_wt_st, 16)
            sp.wait_ge(s_wt_st, 16)
            sp.wait_ge(s_fw, 2)
            out_t = out.rearrange("(n p) d -> p n d", p=P)
            with sp.Fori(0, NB // 2) as pair:
                for k in range(2):
                    tb = Head(pair, k)
                    n = fixed(index(tb) * TB)
                    wait(sp, s_c, tb.count(2 * E + 2, -2 * E - 3))
                    sp.dma_start(spread[k].rearrange("p (e t) -> p e t", e=E),
                                 wt_dram[:, bass.ds(n, TB)].partition_broadcast(P)
                                 ).then_inc(s_wb[k], 16)
                for k in range(2):
                    tb = Head(pair, k)
                    n = bass.ds(fixed(index(tb) * TPB), TPB)
                    wait(sp, s_out, tb.count(1, 1))
                    sp.dma_start(out_t[:, n, :], xt[:, n, :]).then_inc(s_st, 16)
            sp.wait_ge(s_st, 16 * NB)


def slopes():
    start = 2.0 ** (-8.0 / H)
    return [start * start ** i for i in range(H)]


def kernel(**inputs):
    import numpy as np
    import concourse.bacc as bacc
    from concourse.bass_utils import run_bass_kernel_spmd

    a = {k: np.asarray(v) for k, v in inputs.items()}
    f = np.float32
    inv = f(1.0) / (f(10000.0) ** (np.arange(0, DH, 2, dtype=f) / f(DH)))
    angle = np.outer(inv, np.arange(T, dtype=f)).astype(f).astype(np.float64)
    cos, sin = np.cos(angle), np.sin(angle)
    scale = 1.0 / np.sqrt(3.0 * DH)
    cos2, sin2 = np.concatenate([cos, cos]), np.concatenate([-sin, sin])
    cossin = np.stack([np.concatenate([cos2 * scale, cos2]), np.concatenate([sin2 * scale, sin2])], 1).astype(f)
    pos, one = np.arange(T, dtype=f), np.ones(T, f)
    ext = np.stack([np.stack([pos, one, pos, one]), np.stack([one, -pos, one, -pos])])
    c = (np.array(slopes()).astype(f) * f(8.0)).astype(f)
    c_hi = (c.view(np.uint32) & np.uint32(0xFFFFF000)).view(f)
    c_lo = c - c_hi
    ones_h = np.ones(H, f)
    ext_scale = np.stack([np.stack([ones_h, c_hi, ones_h, c_lo]), np.stack([c_hi, ones_h, c_lo, ones_h])])
    i, j = np.meshgrid(np.arange(P), np.arange(P), indexing="ij")
    consts = np.stack([(i == j) * 1.0, (j > i) * -1e9, (i > j) * -1e9], 1).astype(f)

    wq = a["L0_attn_w_qkv"]
    bq = a["L0_attn_b_qkv"]
    swap = np.r_[32:64, 0:32, 96:128, 64:96]
    arrays = {
        "x": a["L0_attn_x"].reshape(T, D),
        "c_col": a["L0_c"].reshape(D, 1),
        "wmod": a["L0_wmod"],
        "cossin": cossin, "ext": ext, "ext_scale": ext_scale, "consts": consts,
        "wqk": np.concatenate([wq[:, :, 0:128], wq[:, :, swap]], 2).transpose(1, 0, 2),
        "bqk": np.stack([bq[:, 0:128].T, bq[:, swap].T], 1),
        "wv": wq[:, :, 128:192].reshape(D, H * DH),
        "bv": bq[:, 128:192].reshape(8, P).T,
        "wout": a["L0_attn_w_out"].reshape(8, P, D).transpose(1, 0, 2).reshape(P, 8 * D),
        "bout": a["L0_attn_b_out"].reshape(1, D),
        "wg": a["L0_ffn_Wg"],
        "bg": a["L0_ffn_bg"].reshape(E, 1),
        "w1": a["L0_ffn_W1"].transpose(1, 0, 2).reshape(D, E * HID),
        "b1": a["L0_ffn_b1"].reshape(E * HC, P).T,
        "w2": a["L0_ffn_W2"].reshape(E, HC, P, D).transpose(2, 0, 1, 3).reshape(P, E * HC * D),
        "b2": a["L0_ffn_b2"],
    }
    nc = bacc.Bacc("TRN2", target_bir_lowering=False, num_devices=1)
    arrays = {f"in_{k}": np.ascontiguousarray(v) for k, v in arrays.items()}
    args = {k[3:]: nc.dram_tensor(k, v.shape, mybir.dt.from_np(v.dtype), kind="ExternalInput").ap()
            for k, v in arrays.items()}
    args["out"] = nc.dram_tensor("out", (T, D), F32, kind="ExternalOutput").ap()
    build(nc, **args)
    r = run_bass_kernel_spmd(nc, [arrays], core_ids=[0])
    return r.results[0]["out"].reshape(1, T, D)
```

```python
import math
from contextlib import ExitStack

import concourse.bass as bass
from concourse import mybir

F32 = mybir.dt.float32
F32R = mybir.dt.float32r
BF16 = mybir.dt.bfloat16
F16 = mybir.dt.float16
ALU = mybir.AluOpType
ACT = mybir.ActivationFunctionType
AX = mybir.AxisListType

P = 128
T = 2048
D = 128
H = 16
DH = 64
NT = T // P
TB = 512
NB = T // TB
TPB = TB // P
E = 8
HID = 512
HC = HID // P
EPS = 1e-5
QKW = 256
NEXT = 4
KA = DH + NEXT
KM = KA + 1
VW = DH + 1
NF = 4
NP = 8
LOW_LEAD = 1 
LEAD = 3
SHIFT = math.log(32.0)
CREDIT = 64

STEPS = []
for _b in range(NB):
    for _kt in range(TPB * (_b + 1)):
        _d = max(0, _kt - TPB * _b)
        STEPS.append((_b, _kt, TB * _b + P * _d, TB - P * _d))
NS = len(STEPS)
BLOCK_END = [max(n for n, s in enumerate(STEPS) if s[0] == b) + 1 for b in range(NB)]
CHUNKS = []
for _qt in range(NT):
    for _k0 in range(0, P * (_qt + 1), TB):
        _n = min(TB, P * (_qt + 1) - _k0)
        CHUNKS.append((_qt, _k0, _n, _k0 + _n == P * (_qt + 1)))
NC = len(CHUNKS)

PROJ_AT = [1, 4, 7, 10] 
TO_ROPE, TO_SUM, TO_HIGH, TO_LOW = 2, 3, 7, 8 
SPLIT_AT = 20
MAX_FROM, MAX_TO = 9, 30
FINAL_AT, TURN_AT, NEGATE_AT = MAX_TO, MAX_TO + 1, MAX_TO + 2
WIDE_FROM = 12
CHUNK_BANK = [_c % 2 if _c < WIDE_FROM else _c % 4 for _c in range(NC)]
CHUNK_PREV = [max([_p for _p in range(_c) if CHUNK_BANK[_p] == CHUNK_BANK[_c]], default=-1) for _c in range(NC)]
LOW_BY = [int(j % 2 == 1 if j < 12 else j < MAX_TO) for j in range(NS)]
LOW_DONE = [LOW_BY[:_j + 1].count(LOW_BY[_j]) for _j in range(NS)]
LOW_ALL = [LOW_BY.count(0), LOW_BY.count(1)]
CHUNKS_AT = [[] for _ in range(NS)]
for _c in range(NC):
    CHUNKS_AT[MAX_FROM + _c * (MAX_TO - MAX_FROM) // NC].append(_c)


class Head:

    def __init__(self, pair, par):
        self.pair, self.par = pair, par

    def plus(self, n):
        k = self.par + n
        return Head(self.pair + k // 2, k % 2)

    def count(self, per, k):
        return self.pair * (2 * per) + (self.par * per + k + CREDIT)

    def turns(self, per):
        return self.pair * per + (per + CREDIT)


def wait(engine, semaphore, value):
    if not isinstance(value, int) or value > CREDIT:
        engine.wait_ge(semaphore, value)


def build(nc, x, c_col, wmod, cossin, ext, consts, wqk, bqk, wv, bv, wout, bout,
          wg, bg, w1, b1, w2, b2, out):
    ctx = ExitStack()
    with ctx:
        def sb(name, shape, dt):
            return ctx.enter_context(nc.sbuf_tensor(name, shape, dt))

        def ps(name):
            return ctx.enter_context(nc.psum_tensor(name, [P, 2, TB], F32))

        def sem(name):
            return ctx.enter_context(nc.semaphore(name))

        v_dram = nc.dram_tensor("v_scratch", [H, P, NT, 2, DH], F16).ap()
        att_dram = nc.dram_tensor("att_scratch", [T, H * DH], F32).ap()
        ext_dram = nc.dram_tensor("alibi_scratch", [H, 2, NEXT, T], F32R).ap()
        wt_dram = nc.dram_tensor("router_scratch", [E, T], F32).ap()

        psS, psM, psV, psJ = ps("psS"), ps("psM"), ps("psV"), ps("psJ")

        xt = sb("xt", [P, NT, D], F32)
        hTh = sb("hTh", [P, T], F32R)
        hTl = sb("hTl", [P, T], F32R)
        Kx = sb("Kx", [P, 2, T], F32R)
        Qx = sb("Qx", [P, 2, T], F32R)
        Kl = sb("Kl", [P, 2, T], F32R)
        Ql = sb("Ql", [P, 2, T], F32R)
        qk_parts = [sb("qk_parts_0", [P, 2, T], F32R), sb("qk_parts_1", [P, 2, T], F32R)]
        qk = sb("qk", [P, T], F32)
        rope_sin = sb("rope_sin", [P, 2, TB], F32)
        prob = sb("prob", [P, NF, TB], F32)
        cs = sb("cs", [P, 2, T], F32)
        wf = sb("wf", [P, 2, QKW], F32)
        wh = sb("wh", [P, 2, QKW], F32R)
        wl = sb("wl", [P, 2, QKW], F32R)
        bqk_sb = sb("bqk_sb", [P, 2, H], F32)
        v16 = sb("v16", [P, 2, NT, 2 * VW], F16)
        prob_hi = sb("prob_hi", [P, NP, TB], F16)
        prob_lo = sb("prob_lo", [P, NP, TB], F16)
        vscale = sb("vscale", [P, 4], F32)
        att = sb("att", [P, 2, NT, DH], F32)
        eye = sb("eye", [P, P], F32)
        eye16 = sb("eye16", [P, P], BF16)
        maskq = sb("maskq", [P, P], BF16)
        maskk = sb("maskk", [P, P], BF16)
        ones = sb("ones", [P, P], F32)
        mxp = sb("mxp", [P, NT, NB], F32)
        mx = sb("mx", [P, NT], F32)
        negm = sb("negm", [NT, P], F32R)
        rden = sb("rden", [P, TPB], F32)
        ccol = sb("ccol", [P, 4], F32)
        modc = sb("modc", [P, 8], F32)
        ga = sb("ga", [P, D], F32)
        stats = sb("stats", [P, NT, 6], F32)
        mv = sb("mv", [P, NT, 2], F32)
        rstd = sb("rstd", [P, NT], F32)
        brow = sb("brow", [1, 2, D], F32)
        bvc = sb("bvc", [P, 8], F32)
        wg_sb = sb("wg_sb", [P, E], F32)
        bg_sb = sb("bg_sb", [E, 2], F32)
        b1_sb = sb("b1_sb", [P, E * HC], F32)
        b2_sb = sb("b2_sb", [E, D], F32)
        wo_hi = sb("wo_hi", [P, 8 * D], F32R)
        wo_lo = sb("wo_lo", [P, 8 * D], F32R)

        qk_hi, qk_lo = qk_parts[0][:, 0, :], qk_parts[0][:, 1, :]
        stage = qk_parts[1][:].rearrange("p a b -> p (a b)").bitcast(F32)
        short = prob_hi[:, 4:8, :].rearrange("p a b -> p (a b)").bitcast(F32)
        gtmp = short[:, 0:2 * D].rearrange("p (a b) -> p a b", b=D)
        x2 = short[:, 2 * D:4 * D].rearrange("p (a b) -> p a b", b=D)
        xn2 = short[:, 4 * D:6 * D].rearrange("p (a b) -> p a b", b=D)
        masks = short[:, 2 * P:4 * P].rearrange("p (a b) -> p a b", b=P)
        wo_f = stage[:, 0:8 * D]
        w_mod = prob[:, 0:2, :].rearrange("p a b -> p (a b)")[:, 0:6 * D]
        wv_f = att[:, 0, :, :].rearrange("p a b -> p (a b)")
        wv_abs = att[:, 1, :, :].rearrange("p a b -> p (a b)")
        k1h, k1l = (a[:].rearrange("p a b -> p (a b)") for a in (Kx, Qx))
        k2h, k2l = (a[:].rearrange("p a b -> p (a b)") for a in (Kl, Ql))
        w1_f = cs[:].rearrange("p a b -> p (a b)")
        w2_f = stage
        router = qk[0:E, :]
        h2 = prob[:, 0:NB, :].rearrange("p a b -> p (a b)")
        spread = [stage, cs[:].rearrange("p a b -> p (a b)")]
        acc, ctmp = rope_sin[:, 0, :], rope_sin[:, 1, :]
        gacc = att[:, 0, :, :].rearrange("p a b -> p (a b)")[:, 0:TB]

        s_ld = sem("setup_loaded")
        s_ld_tab = sem("tables_loaded")
        s_alibi = sem("alibi_rows_rounded")
        s_alibi_st = sem("alibi_rows_stored")
        s_ld_w1 = sem("expert_weights_1_loaded")
        s_ld_w2 = sem("expert_weights_2_loaded")
        s_v0 = sem("vector_setup_step")
        s_a0 = sem("scalar_setup_step")
        s_p0 = sem("tensor_setup_step")
        s_vproj = sem("value_tile_projected")
        s_vcopy_a = sem("value_tile_copied_by_scalar")
        s_vcopy_v = sem("value_tile_copied_by_vector")
        s_vst = [sem("value_tile_stored_0"), sem("value_tile_stored_1")]
        s_w = [sem("qk_weights_loaded_0"), sem("qk_weights_loaded_1")]
        s_v = [sem("values_loaded_0"), sem("values_loaded_1")]
        s_kx = [sem("high_operands_placed_0"), sem("high_operands_placed_1")]
        s_kq = [sem("low_operands_placed_0"), sem("low_operands_placed_1")]
        s_mrow = [sem("max_row_placed_0"), sem("max_row_placed_1")]
        s_att_st = [sem("attention_stored_0"), sem("attention_stored_1")]
        s_wh = sem("qk_weights_high")
        s_wl = sem("qk_weights_low")
        s_proj = sem("block_projected")
        s_rope = sem("rope_terms")
        s_qk = sem("rope_sum")
        s_hi = sem("qk_high_part")
        s_lo = sem("qk_low_part")
        s_mm = sem("max_chunk_scored")
        s_red = sem("max_chunk_reduced")
        s_m = sem("row_maxima")
        s_mt = sem("row_maxima_turned")
        s_neg = sem("row_maxima_negated")
        s_sc = sem("step_scored")
        s_exp = sem("step_exponentiated")
        s_pl = [sem("step_low_by_vector"), sem("step_low_by_gpsimd")]
        s_pv = sem("step_weighted")
        s_rden = sem("row_sums_inverted")
        s_att = sem("block_normalised")
        looped = [*s_w, *s_v, *s_kx, *s_kq, *s_mrow, *s_att_st, s_wh, s_wl, s_proj, s_rope, s_qk, s_hi, s_lo, s_mm, s_red, s_m, s_mt,
                  s_neg, s_sc, s_exp, *s_pl, s_pv, s_rden, s_att]
        s_at = [sem("attention_tile_loaded_0"), sem("attention_tile_loaded_1")]
        s_atT = sem("attention_tile_turned")
        s_ah = sem("attention_tile_high")
        s_al = sem("attention_tile_low")
        s_y = sem("tile_projected")
        s_x2 = sem("second_norm_step")
        s_xT = sem("normalised_tile_turned")
        s_sq = sem("tile_deviation")
        s_h2 = sem("modulated_tile")
        s_h2h = sem("modulated_block_high")
        s_h2l = sem("modulated_block_low")
        looped += [*s_at, s_atT, s_ah, s_al, s_y, s_x2, s_sq, s_xT, s_h2]
        s_z = sem("router_scored")
        s_ez = sem("router_exp")
        s_r = sem("router_step")
        s_wt_st = sem("router_weights_stored")
        s_wb = [sem("router_weights_spread_0"), sem("router_weights_spread_1")]
        s_fw = sem("expert_weights_split")
        s_fwh = sem("expert_weights_high")
        s_u = sem("hidden_scored")
        s_hf = sem("hidden_relu")
        s_hh = sem("hidden_high")
        s_hl = sem("hidden_low")
        s_dn = sem("hidden_consumed")
        s_o = sem("expert_biases")
        s_c = sem("expert_combined")
        s_yt = sem("output_turned")
        s_out = sem("output_tile")
        s_st = sem("output_stored")
        looped += [*s_wb, s_dn, s_u, s_hf, s_hh, s_hl, s_o, s_c, s_yt, s_out]

        block = ctx.enter_context(nc.Block())
        mark = {}
        ALL = {name: count * H + CREDIT for name, count in
               (("sc", NS), ("exp", NS), ("lo", NB), ("hi", NB), ("rope", 2 * NB), ("att", NB), ("neg", 1), ("pv", NS))}

        def slots(engine, slot):
            slot(Head(-1, 0), False, False, True)
            slot(Head(-1, 1), False, True, True)
            with engine.Fori(0, H // 2 - 1) as pair:
                slot(Head(pair, 0), True, True, True)
                slot(Head(pair, 1), True, True, True)
            slot(Head(H // 2 - 1, 0), True, True, False)
            slot(Head(H // 2 - 1, 1), True, False, False)

        def tiles(engine, step):
            step(Head(0, 0), True, False, False)
            step(Head(0, 1), True, True, False)
            with engine.Fori(1, NT // 2) as pair:
                step(Head(pair, 0), True, True, True)
                step(Head(pair, 1), True, True, True)
            step(Head(NT // 2, 0), False, True, True)
            step(Head(NT // 2, 1), False, False, True)

        def index(h):
            return h.pair * 2 + h.par

        def weights_low(engine, h, j):
            w = STEPS[j][3]
            wait(engine, s_exp, h.count(NS, j + 1))
            wait(engine, s_pv, h.count(NS, j + 1 - NP))
            engine.tensor_tensor(prob_lo[:, j % NP, 0:w], prob[:, j % NF, 0:w], prob_hi[:, j % NP, 0:w],
                                 ALU.subtract).then_inc(s_pl[LOW_BY[j]], 1)

        def chunk_scores(c):
            return (psM, psJ)[CHUNK_BANK[c] // 2][:, CHUNK_BANK[c] % 2, :]

        def hidden(buf, i):
            return buf[:, (i % 4) * TB:(i % 4 + 1) * TB]

        setup_loads = [
            (xt[:], x.rearrange("(n p) d -> p n d", p=P)), (ccol[:, 0:1], c_col), (w_mod, wmod),
            (eye[:], consts[:, 0, :]), (masks, consts[:, 1:3, :]), (wv_f, wv), (wo_f, wout), (bvc[:], bv), (brow[:, 0, :], bout),
            (bqk_sb[:], bqk), (wg_sb[:], wg), (bg_sb[:, 0:1], bg), (b1_sb[:], b1), (b2_sb[:], b2)]
        table_loads = [(stage[:, T:2 * T], ext.rearrange("h s r t -> (h s r) t")), (cs[:], cossin)]

        @block.vector
        def _(dve):
            n = [0]

            def link(ins, name=None):
                n[0] += 1
                ins.then_inc(s_v0, 1)
                dve.wait_ge(s_v0, n[0])
                if name:
                    mark[name] = n[0]

            link(dve.memset(ones[:], 1.0))
            link(dve.memset(mxp[:], -3.0e38))
            link(dve.memset(v16[:], 1.0))
            for par in range(2):
                link(dve.memset(Kx[64:96, par, :].bitcast(F32), 1.0), "ones")
            dve.wait_ge(s_ld, 16 * len(setup_loads))
            link(dve.tensor_copy(eye16[:], eye[:]))
            link(dve.tensor_copy(maskq[:], masks[:, 0, :]))
            link(dve.tensor_copy(maskk[:], masks[:, 1, :]))
            dve.wait_ge(s_a0, 1)
            link(dve.tensor_scalar(ccol[:, 2:3], ccol[:, 1:2], 1.0, None, ALU.add))
            link(dve.reciprocal(ccol[:, 3:4], ccol[:, 2:3]))
            link(dve.tensor_tensor(ccol[:, 1:2], ccol[:, 0:1], ccol[:, 3:4], ALU.mult))
            link(dve.tensor_scalar(gtmp[:, 0, :], ones[:], ccol[:, 1:2], None, ALU.mult), "silu")
            for t in range(NT):
                dve.bn_stats(stats[:, t, :], xt[:, t, :]).then_inc(s_v0, 1)
            n[0] += NT
            dve.wait_ge(s_v0, n[0])
            for t in range(NT):
                dve.bn_aggr(mv[:, t, :], stats[:, t, :]).then_inc(s_v0, 1)
            n[0] += NT
            dve.wait_ge(s_v0, n[0])
            link(dve.tensor_scalar(rstd[:], mv[:, :, 1], EPS, None, ALU.add), "var")
            dve.wait_ge(s_a0, 2)
            link(dve.reciprocal(rstd[:], rstd[:]))
            for t in range(NT):
                dve.tensor_scalar(qk[:, t * D:(t + 1) * D], xt[:, t, :], mv[:, t, 0:1], rstd[:, t:t + 1],
                                  ALU.subtract, ALU.mult).then_inc(s_v0, 1)
                n[0] += 1
                mark["xn", t] = n[0]
            dve.wait_ge(s_p0, 1)
            link(dve.tensor_copy(modc[:, 0:6], psJ[:, 0, 0:6]))
            link(dve.tensor_scalar(modc[:, 1:2], modc[:, 1:2], 1.0, None, ALU.add))
            link(dve.tensor_scalar(modc[:, 4:5], modc[:, 4:5], 1.0, None, ALU.add))
            link(dve.tensor_copy(ga[:], psJ[:, 1, 0:D]), "mod")
            for g, sg, mg in ((ga[:], gtmp[:, 0, :], gtmp[:, 1, :]),
                              (modc[:, 5:6], ccol[:, 2:3], ccol[:, 3:4])):
                link(dve.tensor_scalar(sg, g, 0.0, 2.0, ALU.is_ge, ALU.mult))
                link(dve.tensor_scalar(sg, sg, -1.0, None, ALU.add))
                link(dve.tensor_tensor(mg, g, sg, ALU.mult))
                link(dve.scalar_tensor_tensor(g, mg, 0.25, sg, ALU.max, ALU.mult))
            link(dve.tensor_scalar(bg_sb[:, 1:2], bg_sb[:, 0:1], -1.0, None, ALU.mult), "bg")
            for b in range(NB):
                dve.wait_ge(s_p0, 2 + b)
                if b >= 2:
                    dve.wait_ge(s_a0, b + 1)
                link(dve.tensor_scalar(rope_sin[:, b % 2, :], psS[:, b % 2, :], modc[:, 1:2], modc[:, 0:1],
                                       ALU.mult, ALU.add), ("hT", b))
                dve.wait_ge(s_a0, 3 + b)
                link(dve.tensor_tensor(hTl[:, b * TB:(b + 1) * TB], rope_sin[:, b % 2, :],
                                       hTh[:, b * TB:(b + 1) * TB], ALU.subtract), ("hTl", b))
            bound = ccol[:, 2:3]
            link(dve.tensor_scalar(ccol[:, 3:4], modc[:, 1:2], -1.0, None, ALU.mult))
            link(dve.tensor_tensor(bound, modc[:, 1:2], ccol[:, 3:4], ALU.max))
            link(dve.tensor_scalar(ccol[:, 3:4], modc[:, 0:1], -1.0, None, ALU.mult))
            link(dve.tensor_tensor(ccol[:, 3:4], modc[:, 0:1], ccol[:, 3:4], ALU.max))
            link(dve.scalar_tensor_tensor(bound, bound, math.sqrt(D), ccol[:, 3:4], ALU.mult, ALU.add))
            link(dve.tensor_scalar(gtmp[:, 0, :], ones[:], bound, None, ALU.mult))
            link(dve.scalar_tensor_tensor(wv_abs, wv_f, -1.0, wv_f, ALU.mult, ALU.max), "bound")
            dve.wait_ge(s_p0, 6)
            link(dve.tensor_reduce(vscale[:, 0:1], psM[:].rearrange("p a b -> p (a b)"), AX.X, ALU.max))
            link(dve.tensor_scalar(vscale[:, 1:2], vscale[:, 0:1], 1e-30, 2.0 ** -15, ALU.max, ALU.mult))
            link(dve.reciprocal(vscale[:, 2:3], vscale[:, 1:2]), "scale")
            dve.wait_ge(s_p0, 7)
            link(dve.tensor_tensor(brow[:, 1, :], psJ[0:1, 0, 0:D], brow[:, 0, :], ALU.add), "brow")
            link(dve.tensor_scalar(wo_f, wo_f, vscale[:, 1:2], None, ALU.mult), "wout")
            dve.wait_ge(s_a0, 7)
            link(dve.tensor_tensor(qk_lo[:, 0:H * DH], wv_f, qk_hi[:, 0:H * DH], ALU.subtract), "wvl")
            dve.wait_ge(s_a0, 8)
            link(dve.tensor_tensor(wo_lo[:], wo_f, wo_hi[:], ALU.subtract), "wol")
            for t in range(NT):
                k = t % 2
                dve.wait_ge(s_vcopy_a, t + 1)
                if t >= 2:
                    dve.wait_ge(s_vst[k], 32 * (t // 2))
                dve.scalar_tensor_tensor(prob_lo[:, 2 * k:2 * k + 2, :], (psV if k else psM)[:],
                                         vscale[:, 2:3], prob_hi[:, 2 * k:2 * k + 2, :], ALU.mult,
                                         ALU.subtract).then_inc(s_vcopy_v, 1)
            dve.wait_ge(s_ld_tab, 16 * len(table_loads))

            def rope(g, b):
                t = slice(b * TB, (b + 1) * TB)
                wait(dve, s_proj, g.count(NB, b + 1))
                wait(dve, s_lo, g.count(NB, b + 1 - NB))
                dve.scalar_tensor_tensor(qk[:, t], psJ[:, 0, :], bqk_sb[:, 0, bass.ds(index(g), 1)],
                                         cs[:, 0, t], ALU.add, ALU.mult).then_inc(s_rope, 1)
                wait(dve, s_qk, g.count(NB, b - 1))
                dve.scalar_tensor_tensor(rope_sin[:, b % 2, :], psJ[:, 1, :],
                                         bqk_sb[:, 1, bass.ds(index(g), 1)], cs[:, 1, t],
                                         ALU.add, ALU.mult).then_inc(s_rope, 1)

            def reduce_chunk(g, c):
                qt, k0, w, _ = CHUNKS[c]
                wait(dve, s_mm, g.count(NC, c + 1))
                if c == 0:
                    wait(dve, s_m, g.count(1, 0))
                dve.tensor_reduce(mxp[:, qt, k0 // TB:k0 // TB + 1], chunk_scores(c)[:, 0:w], AX.X,
                                  ALU.max).then_inc(s_red, 1)

            def maxima(g):
                wait(dve, s_red, g.count(NC, NC))
                dve.tensor_reduce(mx[:], mxp[:], AX.X, ALU.max).then_inc(s_m, 1)

            def negate(g):
                wait(dve, s_mt, g.count(1, 1))
                wait(dve, s_mrow[g.plus(-1).par], g.plus(-1).turns(16))
                dve.tensor_scalar(negm[:], psM[0:NT, 0, 0:P], -1.0, SHIFT, ALU.mult,
                                  ALU.add).then_inc(s_neg, 1)

            def normalise(h, b):
                wait(dve, s_pv, h.count(NS, BLOCK_END[b]))
                wait(dve, s_att, h.count(NB, b))
                vals = psV[:, b % 2, 0:TPB * VW].rearrange("p (t w) -> p t w", w=VW)
                dve.reciprocal(rden[:], vals[:, :, DH]).then_inc(s_rden, 1)
                wait(dve, s_rden, h.count(NB, b + 1))
                if b == 0:
                    wait(dve, s_att_st[h.par], h.plus(-2).turns(16))
                dve.tensor_tensor(att[:, h.par, b * TPB:(b + 1) * TPB, :], vals[:, :, 0:DH],
                                  rden[:].unsqueeze(2).to_broadcast([P, TPB, DH]),
                                  ALU.mult).then_inc(s_att, 1)

            def slot(h, attend, maximum, project):
                for j in range(NS):
                    if attend and j + LOW_LEAD < NS and LOW_BY[j + LOW_LEAD] == 0:
                        weights_low(dve, h, j + LOW_LEAD)
                    if attend and j - 1 in BLOCK_END:
                        normalise(h, BLOCK_END.index(j - 1))
                    if project and j - TO_ROPE in PROJ_AT:
                        rope(h.plus(2), PROJ_AT.index(j - TO_ROPE))
                    if maximum:
                        for c in CHUNKS_AT[j]:
                            reduce_chunk(h.plus(1), c)
                        if j == FINAL_AT:
                            maxima(h.plus(1))
                        if j == NEGATE_AT:
                            negate(h.plus(1))
                if maximum:
                    for j in range(LOW_LEAD):
                        if LOW_BY[j] == 0:
                            weights_low(dve, h.plus(1), j)
                if attend:
                    normalise(h, NB - 1)

            slots(dve, slot)

            def low_tile(t):
                k = t.par
                wait(dve, s_ah, t.count(1, 1))
                wait(dve, s_y, t.count(1, -1))
                dve.tensor_tensor(qk_lo[:, k * 1024:(k + 1) * 1024],
                                  (psM if k else psS)[:].rearrange("p a b -> p (a b)"),
                                  qk_hi[:, k * 1024:(k + 1) * 1024], ALU.subtract).then_inc(s_al, 1)

            def norm_tile(t):
                k = t.par
                step = [0]

                def then(ins, needed=True):
                    step[0] += 1
                    ins.then_inc(s_x2, 1)
                    if needed:
                        wait(dve, s_x2, t.count(8, step[0]))

                wait(dve, s_y, t.count(1, 1))
                xcur = xt[:, bass.ds(index(t), 1), :].rearrange("p a b -> p (a b)")
                then(dve.tensor_tensor(gtmp[:, k, :], psV[:, k, 0:D], ga[:], ALU.mult))
                then(dve.tensor_tensor(x2[:, k, :], gtmp[:, k, :], xcur, ALU.add))
                then(dve.bn_stats(stats[:, k, :], x2[:, k, :]))
                then(dve.tensor_scalar(xcur, x2[:, k, :], 1.0, None, ALU.mult), False)
                then(dve.bn_aggr(mv[:, k, :], stats[:, k, :]))
                then(dve.tensor_scalar(rstd[:, k:k + 1], mv[:, k, 1:2], EPS, None, ALU.add))
                wait(dve, s_sq, t.count(1, 1))
                then(dve.reciprocal(rstd[:, k:k + 1], rstd[:, k:k + 1]))
                wait(dve, s_xT, t.count(1, -1))
                dve.tensor_scalar(xn2[:, k, :], x2[:, k, :], mv[:, k, 0:1], rstd[:, k:k + 1],
                                  ALU.subtract, ALU.mult).then_inc(s_x2, 1)

            def modulate_tile(t):
                wait(dve, s_xT, t.count(1, 1))
                dve.tensor_scalar(h2[:, bass.ds(index(t) * P, P)], psJ[:, t.par, 0:P], modc[:, 4:5],
                                  modc[:, 3:4], ALU.mult, ALU.add).then_inc(s_h2, 1)

            def tile_step(t, turn, project, modulate):
                if turn:
                    low_tile(t)
                if project:
                    norm_tile(t.plus(-1))
                if modulate:
                    modulate_tile(t.plus(-2))

            tiles(dve, tile_step)

            for b in range(NB):
                t = slice(b * TB, (b + 1) * TB)
                dve.wait_ge(s_ez, b + 1)
                dve.tensor_scalar(router[:, t], router[:, t], 1.0, None, ALU.add).then_inc(s_r, 1)
                dve.wait_ge(s_r, 3 * b + 1)
                dve.reciprocal(router[:, t], router[:, t]).then_inc(s_r, 1)
                dve.wait_ge(s_r, 3 * b + 2)
                dve.scalar_tensor_tensor(router[:, t], router[:, t], 0.5, router[:, t], ALU.is_gt,
                                         ALU.mult).then_inc(s_r, 1)

            def hidden_low(tb, i):
                wait(dve, s_hf, tb.count(E * HC, i + 1))
                wait(dve, s_hh, tb.count(E * HC, i + 1))
                wait(dve, s_dn, tb.count(E * HC, i - 3))
                dve.tensor_tensor(hidden(qk_lo, i), prob[:, i % 4, :], hidden(qk_hi, i),
                                  ALU.subtract).then_inc(s_hl, 1)

            def combine(tb, e):
                wait(dve, s_dn, tb.count(E * HC, HC * (e + 1)))
                wait(dve, s_c, tb.count(2 * E + 2, 2 * e + 1))
                dve.tensor_tensor(ctmp, psV[:, (e + 1) % 2, :], spread[tb.par][:, e * TB:(e + 1) * TB],
                                  ALU.mult).then_inc(s_c, 1)
                wait(dve, s_c, tb.count(2 * E + 2, 2 * e + 2))
                dve.tensor_tensor(acc, acc, ctmp, ALU.add).then_inc(s_c, 1)

            with dve.Fori(0, NB // 2) as pair:
                for k in range(2):
                    tb = Head(pair, k)
                    wait(dve, s_o, tb.count(1, 1))
                    wait(dve, s_c, tb.count(2 * E + 2, 0))
                    dve.tensor_copy(acc, psV[:, 0, :]).then_inc(s_c, 1)
                    for i in range(E * HC):
                        hidden_low(tb, i)
                        if i == 6:
                            wait(dve, s_wb[k], tb.turns(16))
                        if i >= 6 and (i - 6) % HC == 0:
                            combine(tb, (i - 6) // HC)
                    combine(tb, E - 1)
                    wait(dve, s_c, tb.count(2 * E + 2, 2 * E + 1))
                    wait(dve, s_yt, tb.count(1, 0))
                    dve.tensor_scalar(gacc, acc, modc[:, 5:6], None, ALU.mult).then_inc(s_c, 1)
                    wait(dve, s_yt, tb.count(1, 1))
                    xb = xt[:, bass.ds(index(tb) * TPB, TPB), :].rearrange("p a b -> p (a b)")
                    dve.tensor_tensor(xb, psJ[:, k, :], xb, ALU.add).then_inc(s_out, 1)

        @block.scalar
        def _(act):
            act.wait_ge(s_ld, 16 * len(setup_loads))
            act.activation(ccol[:, 1:2], ccol[:, 0:1], ACT.Exp, scale=-1.0).then_inc(s_a0, 1)
            act.wait_ge(s_ld_tab, 16 * len(table_loads))
            act.copy(Kl[:, 0, :], stage[:, T:2 * T]).then_inc(s_alibi, 1)
            act.wait_ge(s_v0, mark["var"])
            act.activation(rstd[:], rstd[:], ACT.Sqrt).then_inc(s_a0, 1)
            for b in range(NB):
                act.wait_ge(s_v0, mark["hT", b])
                act.copy(hTh[:, b * TB:(b + 1) * TB], rope_sin[:, b % 2, :]).then_inc(s_a0, 1)
            act.copy(qk_hi[:, 0:H * DH], wv_f).then_inc(s_a0, 1)
            act.wait_ge(s_v0, mark["wout"])
            act.copy(wo_hi[:], wo_f).then_inc(s_a0, 1)
            for t in range(NT):
                act.wait_ge(s_vproj, t + 1)
                k = t % 2
                if t >= 2:
                    act.wait_ge(s_vst[k], 32 * (t // 2))
                act.activation(prob_hi[:, 2 * k:2 * k + 2, :], (psV if k else psM)[:], ACT.Copy,
                               scale=vscale[:, 2:3]).then_inc(s_vcopy_a, 1)
            for par in range(2):
                act.wait_ge(s_vst[par], 32 * NT // 2)

            def weights_high(g):
                wait(act, s_w[g.par], g.turns(16))
                wait(act, s_proj, g.count(NB, -NB))
                act.copy(wh[:, g.par, :], wf[:, g.par, :]).then_inc(s_wh, 1)

            def high(g, b):
                t = slice(b * TB, (b + 1) * TB)
                wait(act, s_qk, g.count(NB, b + 1))
                if b == 0:
                    wait(act, s_kx[g.par], g.plus(-2).turns(64))
                    wait(act, s_kq[g.par], g.plus(-2).turns(64))
                act.copy(qk_parts[g.par][:, 0, t], qk[:, t]).then_inc(s_hi, 1)

            def exponentiate(h, j):
                w = STEPS[j][3]
                wait(act, s_sc, h.count(NS, j + 1))
                wait(act, s_pv, h.count(NS, j + 1 - NP))
                g, i = (h, j - NF) if j >= NF else (h.plus(-1), j - NF + NS)
                wait(act, s_pl[LOW_BY[i]], g.count(LOW_ALL[LOW_BY[i]], LOW_DONE[i]))
                act.activation(prob[:, j % NF, 0:w], psS[:, j % 2, 0:w], ACT.Exp)
                act.activation(prob_hi[:, j % NP, 0:w], psS[:, j % 2, 0:w], ACT.Exp).then_inc(s_exp, 1)

            def slot(h, attend, maximum, project):
                for j in range(NS):
                    if attend:
                        exponentiate(h, j)
                    if project and j == SPLIT_AT:
                        weights_high(h.plus(3))
                    if project and j - TO_HIGH in PROJ_AT:
                        high(h.plus(2), PROJ_AT.index(j - TO_HIGH))

            weights_high(Head(0, 0))
            slots(act, slot)

            act.wait_ge(s_sc, ALL["sc"])
            act.wait_ge(s_ld_w1, 16)
            act.copy(k1h, w1_f).then_inc(s_fwh, 1)
            act.wait_ge(s_ld_w2, 16)
            act.copy(k2h, w2_f).then_inc(s_fwh, 1)

            def tile_step(t, turn, project, modulate):
                if turn:
                    k = t.par
                    wait(act, s_atT, t.count(1, 1))
                    wait(act, s_y, t.count(1, -1))
                    act.copy(qk_hi[:, k * 1024:(k + 1) * 1024],
                             (psM if k else psS)[:].rearrange("p a b -> p (a b)")).then_inc(s_ah, 1)
                if project:
                    n = t.plus(-1)
                    wait(act, s_x2, n.count(8, 6))
                    act.activation(rstd[:, n.par:n.par + 1], rstd[:, n.par:n.par + 1],
                                   ACT.Sqrt).then_inc(s_sq, 1)

            tiles(act, tile_step)

            act.wait_ge(s_h2, NT + CREDIT)
            for b in range(NB):
                act.copy(hTh[:, b * TB:(b + 1) * TB], h2[:, b * TB:(b + 1) * TB]).then_inc(s_h2h, 1)
                act.wait_ge(s_z, b + 1)
                act.activation(router[:, b * TB:(b + 1) * TB], psJ[0:E, b % 2, :], ACT.Exp,
                               bias=bg_sb[:, 1:2], scale=-1.0).then_inc(s_ez, 1)

            with act.Fori(0, NB // 2) as pair:
                for k in range(2):
                    tb = Head(pair, k)
                    for i in range(E * HC):
                        u = (psS, psM)[i % 4 // 2][:, i % 2, :]
                        wait(act, s_u, tb.count(E * HC, i + 1))
                        wait(act, s_hl, tb.count(E * HC, i - 3))
                        act.activation(prob[:, i % 4, :], u, ACT.Relu,
                                       bias=b1_sb[:, i:i + 1]).then_inc(s_hf, 1)
                        wait(act, s_dn, tb.count(E * HC, i - 3))
                        act.activation(hidden(qk_hi, i), u, ACT.Relu,
                                       bias=b1_sb[:, i:i + 1]).then_inc(s_hh, 1)

        @block.gpsimd
        def _(pool):
            pool.wait_ge(s_vproj, NT)

            def projection_weights_low(g):
                wait(pool, s_wh, g.count(1, 1))
                wait(pool, s_w[g.par], g.turns(16))
                wait(pool, s_proj, g.count(NB, -NB))
                pool.tensor_tensor(wl[:, g.par, :], wf[:, g.par, :], wh[:, g.par, :],
                                   ALU.subtract).then_inc(s_wl, 1)

            def sum_block(g, b):
                t = slice(b * TB, (b + 1) * TB)
                wait(pool, s_rope, g.count(2 * NB, 2 * b + 2))
                pool.tensor_tensor(qk[:, t], qk[:, t], rope_sin[:, b % 2, :], ALU.add).then_inc(s_qk, 1)

            def low_block(g, b):
                t = slice(b * TB, (b + 1) * TB)
                wait(pool, s_hi, g.count(NB, b + 1))
                if b == 0:
                    wait(pool, s_kx[g.par], g.plus(-2).turns(64))
                    wait(pool, s_kq[g.par], g.plus(-2).turns(64))
                pool.tensor_tensor(qk_parts[g.par][:, 1, t], qk[:, t], qk_parts[g.par][:, 0, t], ALU.subtract).then_inc(s_lo, 1)

            def slot(h, attend, maximum, project):
                for j in range(NS):
                    if attend and LOW_BY[j]:
                        weights_low(pool, h, j)
                    if project and j == SPLIT_AT:
                        projection_weights_low(h.plus(3))
                    if project and j - TO_SUM in PROJ_AT:
                        sum_block(h.plus(2), PROJ_AT.index(j - TO_SUM))
                    if project and j - TO_LOW in PROJ_AT:
                        low_block(h.plus(2), PROJ_AT.index(j - TO_LOW))

            projection_weights_low(Head(0, 0))
            slots(pool, slot)

            pool.wait_ge(s_fwh, 1)
            pool.wait_ge(s_ld_w1, 16)
            pool.tensor_tensor(k1l, w1_f, k1h, ALU.subtract).then_inc(s_fw, 1)
            pool.wait_ge(s_fwh, 2)
            pool.wait_ge(s_ld_w2, 16)
            pool.tensor_tensor(k2l, w2_f, k2h, ALU.subtract).then_inc(s_fw, 1)
            for b in range(NB):
                t = slice(b * TB, (b + 1) * TB)
                pool.wait_ge(s_h2h, b + 1)
                pool.tensor_tensor(hTl[:, t], h2[:, t], hTh[:, t], ALU.subtract).then_inc(s_h2l, 1)

        @block.tensor
        def _(pe):
            pe.wait_ge(s_ld, 16 * len(setup_loads))
            pe.wait_ge(s_v0, mark["silu"])
            for k in range(6):
                pe.matmul(psJ[:, 0, k:k + 1], w_mod[:, k * D:(k + 1) * D], ccol[:, 1:2],
                          start=(k == 0), stop=True, skip_group_check=True)
            pe.matmul(psJ[:, 1, 0:D], gtmp[:, 0, :], w_mod[:, 2 * D:3 * D],
                      start=True, stop=True).then_inc(s_p0, 1)
            for b in range(NB):
                if b >= 2:
                    pe.wait_ge(s_v0, mark["hT", b - 2])
                for t in range(TPB * b, TPB * (b + 1)):
                    pe.wait_ge(s_v0, mark["xn", t])
                    mm = pe.transpose(psS[:, b % 2, (t % TPB) * P:(t % TPB + 1) * P],
                                      qk[:, t * P:(t + 1) * P], eye[:])
                mm.then_inc(s_p0, 1)
            pe.wait_ge(s_v0, mark["bound"])
            for c in range(2):
                mm = pe.matmul(psM[:, c, :], gtmp[:, 0, :], wv_abs[:, c * TB:(c + 1) * TB],
                               start=True, stop=True)
            mm.then_inc(s_p0, 1)
            for c in range(8):
                mm = pe.matmul(psJ[0:1, 0, 0:D], bvc[:, c:c + 1], wo_f[:, c * D:(c + 1) * D],
                               start=(c == 0), stop=(c == 7))
            mm.then_inc(s_p0, 1)
            pe.wait_ge(s_v0, mark["wol"])
            for t in range(NT):
                if t >= 2:
                    pe.wait_ge(s_vcopy_a, t - 1)
                    pe.wait_ge(s_vcopy_v, t - 1)
                tt = slice(t * P, (t + 1) * P)
                for c in range(2):
                    cc = slice(c * TB, (c + 1) * TB)
                    o = (psV if t % 2 else psM)[:, c, :]
                    pe.matmul(o, hTh[:, tt], qk_hi[:, cc], start=True, stop=False)
                    pe.matmul(o, hTh[:, tt], qk_lo[:, cc], start=False, stop=False)
                    mm = pe.matmul(o, hTl[:, tt], qk_hi[:, cc], start=False, stop=True)
                mm.then_inc(s_vproj, 1)
            pe.wait_ge(s_vcopy_a, NT)
            pe.wait_ge(s_vcopy_v, NT)
            pe.wait_ge(s_v0, mark["brow"])

            def project(g, b):
                t = slice(b * TB, (b + 1) * TB)
                if b == 0:
                    wait(pe, s_wh, g.count(1, 1))
                    wait(pe, s_wl, g.count(1, 1))
                wait(pe, s_rope, g.count(2 * NB, 2 * b))
                for half in range(2):
                    o, c = psJ[:, half, :], slice(half * P, (half + 1) * P)
                    pe.matmul(o, wh[:, g.par, c], hTh[:, t], start=True, stop=False)
                    pe.matmul(o, wl[:, g.par, c], hTh[:, t], start=False, stop=False)
                    mm = pe.matmul(o, wh[:, g.par, c], hTl[:, t], start=False, stop=True)
                mm.then_inc(s_proj, 1)

            def max_chunk(g, c, projecting):
                qt, k0, w, diagonal = CHUNKS[c]
                if c == 0:
                    wait(pe, s_kx[g.par], g.turns(64))
                    wait(pe, s_neg, g.count(1, 0))
                if CHUNK_PREV[c] >= 0:
                    wait(pe, s_red, g.count(NC, CHUNK_PREV[c] + 1))
                elif CHUNK_BANK[c] >= 2 and projecting:
                    wait(pe, s_rope, g.plus(1).count(2 * NB, 2 * NB))
                mm = pe.matmul(chunk_scores(c)[:, 0:w], Qx[0:KA, g.par, qt * P:(qt + 1) * P],
                               Kx[0:KA, g.par, k0:k0 + w], start=True, stop=True)
                if diagonal:
                    mm = pe.matmul(chunk_scores(c)[:, w - P:w], eye16[:], maskq[:], start=False, stop=True,
                                   skip_group_check=True)
                mm.then_inc(s_mm, 1)

            def turn_maxima(g):
                wait(pe, s_m, g.count(1, 1))
                pe.transpose(psM[0:NT, 0, 0:P], mx[:], eye[:]).then_inc(s_mt, 1)

            def score(h, j, place_next=False):
                b, kt, q0, w = STEPS[j]
                k = slice(kt * P, (kt + 1) * P)
                if j == 0:
                    wait(pe, s_kq[h.par], h.turns(64))
                    wait(pe, s_mrow[h.par], h.turns(16))
                if j == NS - 1 and place_next:
                    wait(pe, s_lo, h.plus(2).count(NB, NB))
                wait(pe, s_exp, h.count(NS, j - 1))
                o = psS[:, j % 2, 0:w]
                pe.matmul(o, Kx[0:KM, h.par, k], Qx[0:KM, h.par, q0:q0 + w], start=True, stop=False)
                if kt >= TPB * b:
                    pe.matmul(psS[:, j % 2, 0:P], eye16[:], maskk[:], start=False, stop=False,
                              skip_group_check=True)
                mm = pe.matmul(o, Kl[:, h.par, k], Ql[:, h.par, q0:q0 + w], start=False, stop=True)
                mm.then_inc(s_sc, 1)

            def weigh(h, j):
                b, kt, q0, w = STEPS[j]
                if j == 0:
                    wait(pe, s_v[h.par], h.turns(32))
                if kt == 0:
                    wait(pe, s_att, h.count(NB, b - 1))
                wait(pe, s_pl[LOW_BY[j]], h.count(LOW_ALL[LOW_BY[j]], LOW_DONE[j]))
                first = (q0 - b * TB) // P
                for t in range(first, TPB):
                    c = slice((t - first) * P, (t - first + 1) * P)
                    hi, lo = prob_hi[:, j % NP, c], prob_lo[:, j % NP, c]
                    v = v16[:, h.par, kt, :]
                    o = psV[:, b % 2, t * VW:(t + 1) * VW]
                    pe.matmul(o, hi, v[:, 0:VW], start=(kt == 0 and t == 0), stop=False,
                              skip_group_check=True)
                    pe.matmul(o[:, 0:DH], hi, v[:, VW:VW + DH], start=False, stop=False,
                              skip_group_check=True)
                    mm = pe.matmul(o, lo, v[:, 0:VW], start=False, stop=(kt == TPB * b + t),
                                   skip_group_check=True)
                mm.then_inc(s_pv, 1)

            def slot(h, attend, maximum, project_):
                for j in range(NS):
                    if attend:
                        if j + LEAD < NS:
                            score(h, j + LEAD, project_)
                        elif maximum:
                            score(h.plus(1), j + LEAD - NS)
                    if project_ and j in PROJ_AT:
                        project(h.plus(2), PROJ_AT.index(j))
                    if maximum:
                        for c in CHUNKS_AT[j][:1]:
                            max_chunk(h.plus(1), c, project_)
                    if attend:
                        weigh(h, j)
                    if maximum:
                        for c in CHUNKS_AT[j][1:]:
                            max_chunk(h.plus(1), c, project_)
                        if j == TURN_AT:
                            turn_maxima(h.plus(1))
                if maximum and not attend:
                    for j in range(LEAD):
                        score(h.plus(1), j)

            slots(pe, slot)
            pe.wait_ge(s_exp, ALL["exp"])
            pe.wait_ge(s_att, ALL["att"])
            pe.wait_ge(s_neg, ALL["neg"])

            def turn_tile(t):
                k = t.par
                wait(pe, s_at[k], t.turns(16))
                wait(pe, s_al, t.count(1, -1))
                for c in range(8):
                    mm = pe.transpose((psM if k else psS)[:, c // 4, (c % 4) * P:(c % 4 + 1) * P],
                                      qk[:, k * 1024 + c * P:k * 1024 + (c + 1) * P], eye[:])
                mm.then_inc(s_atT, 1)

            def out_tile(t):
                k = t.par
                wait(pe, s_al, t.count(1, 1))
                wait(pe, s_x2, t.count(8, -15))
                o = psV[:, k, 0:D]
                pe.matmul(o, ones[0:1, :], brow[:, 1, :], start=True, stop=False)
                for c in range(8):
                    a = slice(k * 1024 + c * P, k * 1024 + (c + 1) * P)
                    w = slice(c * D, (c + 1) * D)
                    pe.matmul(o, qk_hi[:, a], wo_hi[:, w], start=False, stop=False)
                    pe.matmul(o, qk_hi[:, a], wo_lo[:, w], start=False, stop=False)
                    mm = pe.matmul(o, qk_lo[:, a], wo_hi[:, w], start=False, stop=(c == 7))
                mm.then_inc(s_y, 1)

            def turn_norm(t):
                wait(pe, s_x2, t.count(8, 8))
                wait(pe, s_h2, t.count(1, -1))
                pe.transpose(psJ[:, t.par, 0:P], xn2[:, t.par, :], eye[:]).then_inc(s_xT, 1)

            def tile_step(t, turn, project_, modulate):
                if turn:
                    turn_tile(t)
                if project_:
                    out_tile(t.plus(-1))
                if modulate:
                    turn_norm(t.plus(-2))

            tiles(pe, tile_step)

            pe.wait_ge(s_h2, NT + CREDIT)
            for b in range(NB):
                if b >= 2:
                    pe.wait_ge(s_ez, b - 1)
                pe.matmul(psJ[0:E, b % 2, :], wg_sb[:], h2[:, b * TB:(b + 1) * TB],
                          start=True, stop=True).then_inc(s_z, 1)
            pe.wait_ge(s_ez, NB)
            pe.wait_ge(s_r, 3 * NB)
            pe.wait_ge(s_x2, 8 * NT + CREDIT)
            pe.wait_ge(s_fw, 2)
            pe.wait_ge(s_h2l, NB)

            def hidden_scores(tb, i):
                t = bass.ds(index(tb) * TB, TB)
                w = slice(i * P, (i + 1) * P)
                o = (psS, psM)[i % 4 // 2][:, i % 2, :]
                wait(pe, s_hh, tb.count(E * HC, i - 3))
                pe.matmul(o, k1h[:, w], hTh[:, t], start=True, stop=False)
                pe.matmul(o, k1l[:, w], hTh[:, t], start=False, stop=False)
                pe.matmul(o, k1h[:, w], hTl[:, t], start=False, stop=True).then_inc(s_u, 1)

            def expert_out(tb, i):
                e, c = i // HC, i % HC
                w = slice(i * P, (i + 1) * P)
                o = psV[:, (e + 1) % 2, :]
                if c == 0:
                    wait(pe, s_c, tb.count(2 * E + 2, -4 if e == 0 else 1 if e == 1 else 2 * e - 2))
                wait(pe, s_hl, tb.count(E * HC, i + 1))
                pe.matmul(o, k2h[:, w], hidden(qk_hi, i), start=(c == 0), stop=False)
                pe.matmul(o, k2l[:, w], hidden(qk_hi, i), start=False, stop=False)
                mm = pe.matmul(o, k2h[:, w], hidden(qk_lo, i), start=False, stop=(c == HC - 1))
                mm.then_inc(s_dn, 1)
                return mm

            with pe.Fori(0, NB // 2) as pair:
                for k in range(2):
                    tb = Head(pair, k)
                    wait(pe, s_c, tb.count(2 * E + 2, -2))
                    pe.matmul(psV[:, 0, :], b2_sb[:], router[:, bass.ds(index(tb) * TB, TB)],
                              start=True, stop=True).then_inc(s_o, 1)
                    for i in range(E * HC + 3):
                        if i < E * HC:
                            hidden_scores(tb, i)
                        if i >= 3:
                            expert_out(tb, i - 3)
                    wait(pe, s_c, tb.count(2 * E + 2, 2 * E + 2))
                    wait(pe, s_out, tb.count(1, -1))
                    for t in range(TPB):
                        mm = pe.transpose(psJ[:, k, t * P:(t + 1) * P], gacc[:, t * P:(t + 1) * P], eye[:])
                    mm.then_inc(s_yt, 1)

        @block.sync
        def _(sp):
            def fixed(value):
                return value if isinstance(value, int) else sp.snap(value)

            for s in looped:
                sp.sem_inc(s, CREDIT)
            for dst, src in setup_loads:
                sp.dma_start(dst, src).then_inc(s_ld, 16)
            for dst, src in table_loads:
                sp.dma_start(dst, src).then_inc(s_ld_tab, 16)
            sp.wait_ge(s_alibi, 1)
            sp.dma_start(ext_dram.rearrange("h s r t -> (h s r) t").bitcast(F32),
                         Kl[:, 0, :].bitcast(F32)).then_inc(s_alibi_st, 16)
            for t in range(NT):
                sp.wait_ge(s_vcopy_a, t + 1)
                sp.wait_ge(s_vcopy_v, t + 1)
                k = t % 2
                for part, tile in enumerate((prob_hi, prob_lo)):
                    sp.dma_start(v_dram[:, :, t, part, :].rearrange("h p d -> p h d"),
                                 tile[:, 2 * k:2 * k + 2, :].rearrange("p a (h d) -> p (a h) d", d=DH)
                                 ).then_inc(s_vst[k], 16)
            for par in range(2):
                sp.wait_ge(s_vst[par], 32 * NT // 2)
            sp.wait_ge(s_alibi_st, 16)
            sp.wait_ge(s_v0, mark["wol"])

            def load_weights(g):
                n = fixed(index(g))
                wait(sp, s_wl, g.count(1, -1))
                sp.dma_start(wf[:, g.par, :], wqk[bass.ds(n, 1)].rearrange("a p c -> p (a c)")
                             ).then_inc(s_w[g.par], 16)

            def load_values(g):
                n = fixed(index(g))
                wait(sp, s_pv, g.count(NS, -NS))
                for part in range(2):
                    sp.dma_start(v16[:, g.par, :, part * VW:part * VW + DH],
                                 v_dram[bass.ds(n, 1), :, :, part, :].rearrange("a p t d -> p (a t) d")
                                 ).then_inc(s_v[g.par], 16)

            def place(g, attend):
                k = g.par
                n = fixed(index(g))
                if attend:
                    wait(sp, s_sc, g.count(NS, -NS))
                else:
                    wait(sp, s_lo, g.count(NB, NB))
                for rows, side in ((Kx, 0), (Qx, 1)):
                    sp.dma_start(rows[DH:KA, k, :].bitcast(F32),
                                 ext_dram[bass.ds(n, 1), side].rearrange("a r t -> r (a t)").bitcast(F32)).then_inc(s_kx[k], 16)
                hi, lo = qk_parts[k][:, 0, :], qk_parts[k][:, 1, :]
                for done, dst, src in ((s_kx, Kx[0:DH, k, :], hi[DH:P, :]), (s_kx, Qx[0:DH, k, :], hi[0:DH, :]),
                                       (s_kq, Kl[0:DH, k, :], lo[DH:P, :]), (s_kq, Kl[DH:P, k, :], hi[DH:P, :]),
                                       (s_kq, Ql[0:DH, k, :], hi[0:DH, :]), (s_kq, Ql[DH:P, k, :], lo[0:DH, :])):
                    sp.dma_start(dst.bitcast(F32), src.bitcast(F32)).then_inc(done[k], 16)

            def slot(h, attend, maximum, project):
                if project:
                    load_weights(h.plus(3))
                if maximum:
                    load_values(h.plus(1))
                    g = h.plus(1)
                    wait(sp, s_neg, g.count(1, 1))
                    sp.dma_start(Qx[KA:KM, g.par, :].bitcast(F32), negm[:].bitcast(F32)).then_inc(s_mrow[g.par], 16)
                if project:
                    place(h.plus(2), attend)
                if attend:
                    n = fixed(index(h) * DH)
                    wait(sp, s_att, h.count(NB, NB))
                    sp.dma_start(att_dram.rearrange("(n p) c -> p n c", p=P)[:, :, bass.ds(n, DH)],
                                 att[:, h.par, :, :]).then_inc(s_att_st[h.par], 16)

            load_weights(Head(0, 0))
            slots(sp, slot)
            sp.wait_ge(s_rope, ALL["rope"])
            sp.dma_start(w1_f, w1).then_inc(s_ld_w1, 16)
            sp.wait_ge(s_kx[1], 64 * H // 2 + CREDIT)
            sp.wait_ge(s_kq[1], 64 * H // 2 + CREDIT)
            sp.dma_start(w2_f, w2).then_inc(s_ld_w2, 16)
            for par in range(2):
                sp.wait_ge(s_att_st[par], 16 * H // 2 + CREDIT)
            sp.wait_ge(s_lo, ALL["lo"])

            with sp.Fori(0, NT // 2) as pair:
                for k in range(2):
                    t = Head(pair, k)
                    n = fixed(index(t) * P)
                    wait(sp, s_atT, t.count(1, -1))
                    sp.dma_start(qk[:, k * 1024:(k + 1) * 1024],
                                 att_dram[bass.ds(n, P), :]).then_inc(s_at[k], 16)

            sp.wait_ge(s_r, 3 * NB)
            sp.dma_start(wt_dram, router).then_inc(s_wt_st, 16)
            sp.wait_ge(s_wt_st, 16)
            sp.wait_ge(s_fw, 2)
            out_t = out.rearrange("(n p) d -> p n d", p=P)
            with sp.Fori(0, NB // 2) as pair:
                for k in range(2):
                    tb = Head(pair, k)
                    n = fixed(index(tb) * TB)
                    wait(sp, s_c, tb.count(2 * E + 2, -2 * E - 3))
                    sp.dma_start(spread[k].rearrange("p (e t) -> p e t", e=E),
                                 wt_dram[:, bass.ds(n, TB)].partition_broadcast(P)
                                 ).then_inc(s_wb[k], 16)
                for k in range(2):
                    tb = Head(pair, k)
                    n = bass.ds(fixed(index(tb) * TPB), TPB)
                    wait(sp, s_out, tb.count(1, 1))
                    sp.dma_start(out_t[:, n, :], xt[:, n, :]).then_inc(s_st, 16)
            sp.wait_ge(s_st, 16 * NB)


def slopes():
    start = 2.0 ** (-8.0 / H)
    return [start * start ** i for i in range(H)]


def kernel(**inputs):
    import numpy as np
    import concourse.bacc as bacc
    from concourse.bass_utils import run_bass_kernel_spmd

    a = {k: np.asarray(v) for k, v in inputs.items()}
    f = np.float32
    inv = f(1.0) / (f(10000.0) ** (np.arange(0, DH, 2, dtype=f) / f(DH)))
    angle = np.outer(inv, np.arange(T, dtype=f)).astype(f).astype(np.float64)
    cos, sin = np.cos(angle), np.sin(angle)
    scale = 1.0 / np.sqrt(3.0 * DH)
    cos2, sin2 = np.concatenate([cos, cos]), np.concatenate([-sin, sin])
    cossin = np.stack([np.concatenate([cos2 * scale, cos2]), np.concatenate([sin2 * scale, sin2])], 1).astype(f)
    pos, one = np.arange(T, dtype=f), np.ones(T, f)
    c = (np.array(slopes()).astype(f) * f(8.0)).astype(f)
    c_hi = (c.view(np.uint32) & np.uint32(0xFFFFF000)).view(f)
    c_lo = c - c_hi
    ext = np.stack([np.stack([np.stack([pos, hi * one, pos, lo * one]), np.stack([hi * one, -pos, lo * one, -pos])])
                    for hi, lo in zip(c_hi, c_lo)])
    i, j = np.meshgrid(np.arange(P), np.arange(P), indexing="ij")
    consts = np.stack([(i == j) * 1.0, (j > i) * -1e9, (i > j) * -1e9], 1).astype(f)

    wq = a["L0_attn_w_qkv"]
    bq = a["L0_attn_b_qkv"]
    swap = np.r_[32:64, 0:32, 96:128, 64:96]
    arrays = {
        "x": a["L0_attn_x"].reshape(T, D),
        "c_col": a["L0_c"].reshape(D, 1),
        "wmod": a["L0_wmod"],
        "cossin": cossin, "ext": ext, "consts": consts,
        "wqk": np.concatenate([wq[:, :, 0:128], wq[:, :, swap]], 2).transpose(1, 0, 2)[np.r_[0:H, H - 1]],
        "bqk": np.stack([bq[:, 0:128].T, bq[:, swap].T], 1),
        "wv": wq[:, :, 128:192].reshape(D, H * DH),
        "bv": bq[:, 128:192].reshape(8, P).T,
        "wout": a["L0_attn_w_out"].reshape(8, P, D).transpose(1, 0, 2).reshape(P, 8 * D),
        "bout": a["L0_attn_b_out"].reshape(1, D),
        "wg": a["L0_ffn_Wg"],
        "bg": a["L0_ffn_bg"].reshape(E, 1),
        "w1": a["L0_ffn_W1"].transpose(1, 0, 2).reshape(D, E * HID),
        "b1": a["L0_ffn_b1"].reshape(E * HC, P).T,
        "w2": a["L0_ffn_W2"].reshape(E, HC, P, D).transpose(2, 0, 1, 3).reshape(P, E * HC * D),
        "b2": a["L0_ffn_b2"],
    }
    nc = bacc.Bacc("TRN2", target_bir_lowering=False, num_devices=1)
    arrays = {f"in_{k}": np.ascontiguousarray(v) for k, v in arrays.items()}
    args = {k[3:]: nc.dram_tensor(k, v.shape, mybir.dt.from_np(v.dtype), kind="ExternalInput").ap()
            for k, v in arrays.items()}
    args["out"] = nc.dram_tensor("out", (T, D), F32, kind="ExternalOutput").ap()
    build(nc, **args)
    r = run_bass_kernel_spmd(nc, [arrays], core_ids=[0])
    return r.results[0]["out"].reshape(1, T, D)
```

```python
import math
from contextlib import ExitStack

import concourse.bass as bass
from concourse import mybir

F32 = mybir.dt.float32
F32R = mybir.dt.float32r
BF16 = mybir.dt.bfloat16
F16 = mybir.dt.float16
ALU = mybir.AluOpType
ACT = mybir.ActivationFunctionType
AX = mybir.AxisListType

P = 128
T = 2048
D = 128
H = 16
DH = 64
NT = T // P
TB = 512
NB = T // TB
TPB = TB // P
E = 8
HID = 512
HC = HID // P
EPS = 1e-5
QKW = 256
NEXT = 4
KA = DH + NEXT
KM = KA + 1
VW = DH + 1
VR = 4
NF = 4
NP = 8
LOW_LEAD = 1
EXP_LEAD = 3
LEAD = 4
SHIFT = math.log(32.0)
V_AT = 3
XC = 2 * E + 1
XS = 6
CREDIT = 64

STEPS = []
for _b in range(NB):
    for _kt in range(TPB * (_b + 1)):
        _d = max(0, _kt - TPB * _b)
        STEPS.append((_b, _kt, TB * _b + P * _d, TB - P * _d))
NS = len(STEPS)
BLOCK_END = [max(n for n, s in enumerate(STEPS) if s[0] == b) + 1 for b in range(NB)]
CHUNKS = []
for _qt in range(NT):
    for _k0 in range(0, P * (_qt + 1), TB):
        _n = min(TB, P * (_qt + 1) - _k0)
        CHUNKS.append((_qt, _k0, _n, _k0 + _n == P * (_qt + 1)))
NC = len(CHUNKS)

PROJ_AT = [0, 4, 7, 10]
TO_ROPE, TO_SUM, TO_HIGH, TO_LOW = 2, 3, 5, 8
SPLIT_AT = 20
FIRST_PROJ_AT = [2, 5, 8, 11]
MAX_FROM, MAX_TO = 9, 30
FINAL_AT, TURN_AT, NEGATE_AT = MAX_TO, MAX_TO + 1, MAX_TO + 2
WIDE_FROM = 12
CHUNK_BANK = [_c % 2 if _c < WIDE_FROM else _c % 4 for _c in range(NC)]
CHUNK_PREV = [max([_p for _p in range(_c) if CHUNK_BANK[_p] == CHUNK_BANK[_c]], default=-1) for _c in range(NC)]
LOW_BY = [int(j % 2 == 1 if j < 12 else j < MAX_TO and j % 3 != 0) for j in range(NS)]
LOW_DONE = [LOW_BY[:_j + 1].count(LOW_BY[_j]) for _j in range(NS)]
LOW_ALL = [LOW_BY.count(0), LOW_BY.count(1)]
CHUNKS_AT = [[] for _ in range(NS)]
for _c in range(NC):
    CHUNKS_AT[MAX_FROM + _c * (MAX_TO - MAX_FROM) // NC].append(_c)

TURN_LAG = 9
TURNS_AT = [E * HC + TURN_LAG, 2 * E * HC + TURN_LAG]


class Head:

    def __init__(self, pair, par):
        self.pair, self.par = pair, par

    def plus(self, n):
        k = self.par + n
        return Head(self.pair + k // 2, k % 2)

    def count(self, per, k):
        return self.pair * (2 * per) + (self.par * per + k + CREDIT)

    def turns(self, per):
        return self.pair * per + (per + CREDIT)


def wait(engine, semaphore, value):
    if not isinstance(value, int) or value > CREDIT:
        engine.wait_ge(semaphore, value)


def build(nc, x, c_col, wmod, cossin, ext, consts, wqk, bqk, wv, bv, wout, bout,
          wg, bg, w1, b1, w2, b2, out):
    ctx = ExitStack()
    with ctx:
        def sb(name, shape, dt):
            return ctx.enter_context(nc.sbuf_tensor(name, shape, dt))

        def ps(name):
            return ctx.enter_context(nc.psum_tensor(name, [P, 2, TB], F32))

        def sem(name):
            return ctx.enter_context(nc.semaphore(name))

        v_dram = nc.dram_tensor("v_scratch", [P, NT, 2, V_AT + H, DH], F16).ap()
        att_dram = nc.dram_tensor("att_scratch", [T, H * DH], F32).ap()
        ext_dram = nc.dram_tensor("alibi_scratch", [H, 2, NEXT, T], F32R).ap()
        wt_dram = nc.dram_tensor("router_scratch", [E, T], F32).ap()

        psS, psM, psV, psJ = ps("psS"), ps("psM"), ps("psV"), ps("psJ")

        xt = sb("xt", [P, NT, D], F32)
        hTh = sb("hTh", [P, T], F32R)
        hTl = sb("hTl", [P, T], F32R)
        Kx = sb("Kx", [P, 2, T], F32R)
        Qx = sb("Qx", [P, 2, T], F32R)
        Kl = sb("Kl", [P, 2, T], F32R)
        Ql = sb("Ql", [P, 2, T], F32R)
        qk_parts = [sb("qk_parts_0", [P, 2, T], F32R), sb("qk_parts_1", [P, 2, T], F32R)]
        qk = sb("qk", [P, T], F32)
        rope_sin = sb("rope_sin", [P, 2, TB], F32)
        prob = sb("prob", [P, NF, TB], F32)
        cs = sb("cs", [P, 2, T], F32)
        wf = sb("wf", [P, 2, QKW], F32)
        wh = sb("wh", [P, 2, QKW], F32R)
        wl = sb("wl", [P, 2, QKW], F32R)
        bqk_sb = sb("bqk_sb", [P, 2, H], F32)
        v16 = sb("v16", [P, 2, NT, 2 * VW], F16)
        prob_hi = sb("prob_hi", [P, NP, TB], F16)
        prob_lo = sb("prob_lo", [P, NP, TB], F16)
        vscale = sb("vscale", [P, 4], F32)
        att = sb("att", [P, 2, NT, DH], F32)
        eye = sb("eye", [P, P], F32)
        eye16 = sb("eye16", [P, P], BF16)
        maskq = sb("maskq", [P, P], BF16)
        maskk = sb("maskk", [P, P], BF16)
        ones = sb("ones", [P, P], F32)
        eps = sb("eps", [P, 1], F32)
        mxp = sb("mxp", [P, NT, NB], F32)
        mx = sb("mx", [P, NT], F32)
        negm = sb("negm", [NT, P], F32R)
        rden = sb("rden", [P, TPB], F32)
        ccol = sb("ccol", [P, 4], F32)
        modc = sb("modc", [P, 8], F32)
        ga = sb("ga", [P, D], F32)
        stats = sb("stats", [P, NT, 6], F32)
        mv = sb("mv", [P, NT, 2], F32)
        rstd = sb("rstd", [P, NT], F32)
        brow = sb("brow", [1, 2, D], F32)
        bvc = sb("bvc", [P, 8], F32)
        wg_sb = sb("wg_sb", [P, E], F32)
        bg_sb = sb("bg_sb", [E, 2], F32)
        b1_sb = sb("b1_sb", [P, E * HC], F32)
        b2_sb = sb("b2_sb", [E, D], F32)
        wo_hi = sb("wo_hi", [P, 8 * D], F32R)
        wo_lo = sb("wo_lo", [P, 8 * D], F32R)

        qk_hi, qk_lo = qk_parts[0][:, 0, :], qk_parts[0][:, 1, :]
        wv_hi, wv_lo = Ql[:, 0, 0:H * DH], Ql[:, 1, 0:H * DH]
        stage = qk_parts[1][:].rearrange("p a b -> p (a b)").bitcast(F32)
        short = prob_hi[:, 4:8, :].rearrange("p a b -> p (a b)").bitcast(F32)
        gtmp = short[:, 0:2 * D].rearrange("p (a b) -> p a b", b=D)
        x2 = short[:, 2 * D:4 * D].rearrange("p (a b) -> p a b", b=D)
        xn2 = short[:, 4 * D:6 * D].rearrange("p (a b) -> p a b", b=D)
        masks = short[:, 2 * P:4 * P].rearrange("p (a b) -> p a b", b=P)
        wo_f = prob[:, 2:4, :].rearrange("p a b -> p (a b)")
        w_mod = prob[:, 0:2, :].rearrange("p a b -> p (a b)")[:, 0:6 * D]
        wv_f = att[:, 0, :, :].rearrange("p a b -> p (a b)")
        wv_abs = att[:, 1, :, :].rearrange("p a b -> p (a b)")
        k1h, k1l = (a[:].rearrange("p a b -> p (a b)") for a in (Kx, Qx))
        k2h, k2l = (a[:].rearrange("p a b -> p (a b)") for a in (Kl, Ql))
        w1_f = cs[:].rearrange("p a b -> p (a b)")
        w2_f = stage
        router = qk[0:E, :]
        h2 = prob[:, 0:NB, :].rearrange("p a b -> p (a b)")
        spread = [stage, cs[:].rearrange("p a b -> p (a b)")]
        acc, ctmp = rope_sin[:, 0, :], rope_sin[:, 1, :]
        gacc = att[:, 0, :, :].rearrange("p a b -> p (a b)")[:, 0:TB]

        s_ld = sem("setup_loaded")
        s_ld_tab = sem("tables_loaded")
        s_alibi = sem("alibi_rows_rounded")
        s_alibi_st = sem("alibi_rows_stored")
        s_ld_w1 = sem("expert_weights_1_loaded")
        s_ld_w2 = sem("expert_weights_2_loaded")
        s_v0 = sem("vector_setup_step")
        s_a0 = sem("scalar_setup_step")
        s_p0 = sem("tensor_setup_step")
        s_vproj = sem("value_tile_projected")
        s_vcopy_a = sem("value_tile_copied_by_scalar")
        s_vcopy_v = sem("value_tile_copied_by_vector")
        s_vst = [sem(f"value_tile_stored_{k}") for k in range(VR)]
        s_w = [sem("qk_weights_loaded_0"), sem("qk_weights_loaded_1")]
        s_v = [sem("values_loaded_0"), sem("values_loaded_1")]
        s_kx = [sem("high_operands_placed_0"), sem("high_operands_placed_1")]
        s_kq = [sem("low_operands_placed_0"), sem("low_operands_placed_1")]
        s_mrow = [sem("max_row_placed_0"), sem("max_row_placed_1")]
        s_att_st = [sem("attention_stored_0"), sem("attention_stored_1")]
        s_wh = sem("qk_weights_high")
        s_wl = sem("qk_weights_low")
        s_proj = sem("block_projected")
        s_rope = sem("rope_terms")
        s_qk = sem("rope_sum")
        s_hi = sem("qk_high_part")
        s_lo = sem("qk_low_part")
        s_mm = sem("max_chunk_scored")
        s_red = sem("max_chunk_reduced")
        s_m = sem("row_maxima")
        s_mt = sem("row_maxima_turned")
        s_neg = sem("row_maxima_negated")
        s_sc = sem("step_scored")
        s_exp = sem("step_exponentiated")
        s_pl = [sem("step_low_by_vector"), sem("step_low_by_gpsimd")]
        s_pv = sem("step_weighted")
        s_rden = sem("row_sums_inverted")
        s_att = sem("block_normalised")
        looped = [*s_w, *s_v, *s_kx, *s_kq, *s_mrow, *s_att_st, s_wh, s_wl, s_proj,
                  s_rope, s_qk, s_hi, s_lo, s_mm, s_red, s_m, s_mt,
                  s_neg, s_sc, s_exp, *s_pl, s_pv, s_rden, s_att]
        s_at = [sem("attention_tile_loaded_0"), sem("attention_tile_loaded_1")]
        s_atT = sem("attention_tile_turned")
        s_ah = sem("attention_tile_high")
        s_al = sem("attention_tile_low")
        s_y = sem("tile_projected")
        s_x2 = sem("second_norm_step")
        s_xT = sem("normalised_tile_turned")
        s_sq = sem("tile_deviation")
        s_h2 = sem("modulated_tile")
        s_h2h = sem("modulated_block_high")
        s_h2l = sem("modulated_block_low")
        looped += [*s_at, s_atT, s_ah, s_al, s_y, s_x2, s_sq, s_xT, s_h2, s_h2h, s_h2l]
        s_z = sem("router_scored")
        s_ez = sem("router_exp")
        s_r = sem("router_step")
        s_wt_st = sem("router_weights_stored")
        s_wb = [sem("router_weights_spread_0"), sem("router_weights_spread_1")]
        s_fw = sem("expert_weights_split")
        s_fwh = sem("expert_weights_high")
        s_u = sem("hidden_scored")
        s_hf = sem("hidden_relu")
        s_hh = sem("hidden_high")
        s_hl = sem("hidden_low")
        s_dn = sem("hidden_consumed")
        s_o = sem("expert_biases")
        s_c = sem("expert_combined")
        s_yt = sem("output_turned")
        s_out = sem("output_tile")
        s_st = sem("output_stored")
        looped += [*s_wb, s_dn, s_u, s_hf, s_hh, s_hl, s_o, s_c, s_yt, s_out]

        block = ctx.enter_context(nc.Block())
        mark = {}
        ALL = {name: count * H + CREDIT for name, count in
               (("sc", NS), ("exp", NS), ("lo", NB), ("rope", 2 * NB), ("att", NB), ("neg", 1))}

        def slots(engine, slot):
            slot(Head(-1, 1), False, True, True)
            with engine.Fori(0, H // 2 - 1) as pair:
                slot(Head(pair, 0), True, True, True)
                slot(Head(pair, 1), True, True, True)
            slot(Head(H // 2 - 1, 0), True, True, False)
            slot(Head(H // 2 - 1, 1), True, False, False)

        def tiles(engine, step):
            step(Head(0, 0), True, False, False)
            step(Head(0, 1), True, True, False)
            with engine.Fori(1, NT // 2) as pair:
                step(Head(pair, 0), True, True, True)
                step(Head(pair, 1), True, True, True)
            step(Head(NT // 2, 0), False, True, True)
            step(Head(NT // 2, 1), False, False, True)

        def index(h):
            return h.pair * 2 + h.par

        def weights_low(engine, h, j):
            w = STEPS[j][3]
            wait(engine, s_exp, h.count(NS, j + 1))
            wait(engine, s_pv, h.count(NS, j + 1 - NP))
            engine.tensor_tensor(prob_lo[:, j % NP, 0:w], prob[:, j % NF, 0:w], prob_hi[:, j % NP, 0:w],
                                 ALU.subtract).then_inc(s_pl[LOW_BY[j]], 1)

        def chunk_scores(c):
            return (psM, psJ)[CHUNK_BANK[c] // 2][:, CHUNK_BANK[c] % 2, :]

        def hidden(buf, i):
            return buf[:, (i % 4) * TB:(i % 4 + 1) * TB]

        setup_loads = [
            (xt[:], x.rearrange("(n p) d -> p n d", p=P)), (ccol[:, 0:1], c_col), (w_mod, wmod),
            (eye[:], consts[:, 0, :]), (masks, consts[:, 1:3, :]), (wv_f, wv), (wo_f, wout), (bvc[:], bv), (brow[:, 0, :], bout),
            (bqk_sb[:], bqk), (wg_sb[:], wg), (bg_sb[:, 0:1], bg), (b1_sb[:], b1), (b2_sb[:], b2)]
        table_loads = [(stage[:, T:2 * T], ext.rearrange("h s r t -> (h s r) t")), (cs[:], cossin)]

        @block.vector
        def _(dve):
            n = [0]

            def link(ins, name=None):
                n[0] += 1
                ins.then_inc(s_v0, 1)
                dve.wait_ge(s_v0, n[0])
                if name:
                    mark[name] = n[0]

            link(dve.memset(ones[:], 1.0))
            link(dve.memset(eps[:], EPS))
            link(dve.memset(mxp[:], -3.0e38))
            link(dve.memset(v16[:], 1.0))
            for par in range(2):
                link(dve.memset(Kx[64:96, par, :].bitcast(F32), 1.0), "ones")
            dve.wait_ge(s_ld, 16 * len(setup_loads))
            link(dve.tensor_copy(eye16[:], eye[:]))
            link(dve.tensor_copy(maskq[:], masks[:, 0, :]))
            link(dve.tensor_copy(maskk[:], masks[:, 1, :]))
            dve.wait_ge(s_a0, 1)
            link(dve.tensor_scalar(ccol[:, 2:3], ccol[:, 1:2], 1.0, None, ALU.add))
            link(dve.reciprocal(ccol[:, 3:4], ccol[:, 2:3]))
            link(dve.tensor_tensor(ccol[:, 1:2], ccol[:, 0:1], ccol[:, 3:4], ALU.mult))
            link(dve.tensor_scalar(gtmp[:, 0, :], ones[:], ccol[:, 1:2], None, ALU.mult), "silu")
            for t in range(NT):
                dve.bn_stats(stats[:, t, :], xt[:, t, :]).then_inc(s_v0, 1)
            n[0] += NT
            dve.wait_ge(s_v0, n[0])
            for t in range(NT):
                dve.bn_aggr(mv[:, t, :], stats[:, t, :]).then_inc(s_v0, 1)
            n[0] += NT
            dve.wait_ge(s_v0, n[0])
            link(dve.tensor_scalar(rstd[:], mv[:, :, 1], EPS, None, ALU.add), "var")
            dve.wait_ge(s_a0, 2)
            link(dve.reciprocal(rstd[:], rstd[:]))
            for t in range(NT):
                dve.tensor_scalar(qk[:, t * D:(t + 1) * D], xt[:, t, :], mv[:, t, 0:1], rstd[:, t:t + 1],
                                  ALU.subtract, ALU.mult).then_inc(s_v0, 1)
                n[0] += 1
                mark["xn", t] = n[0]
            dve.wait_ge(s_p0, 1)
            link(dve.tensor_copy(modc[:, 0:6], psJ[:, 0, 0:6]))
            link(dve.tensor_scalar(modc[:, 1:2], modc[:, 1:2], 1.0, None, ALU.add))
            link(dve.tensor_scalar(modc[:, 4:5], modc[:, 4:5], 1.0, None, ALU.add))
            link(dve.tensor_copy(ga[:], psJ[:, 1, 0:D]), "mod")
            for g, sg, mg in ((ga[:], gtmp[:, 0, :], gtmp[:, 1, :]),
                              (modc[:, 5:6], ccol[:, 2:3], ccol[:, 3:4])):
                link(dve.tensor_scalar(sg, g, 0.0, 2.0, ALU.is_ge, ALU.mult))
                link(dve.tensor_scalar(sg, sg, -1.0, None, ALU.add))
                link(dve.tensor_tensor(mg, g, sg, ALU.mult))
                link(dve.scalar_tensor_tensor(g, mg, 0.25, sg, ALU.max, ALU.mult))
            link(dve.tensor_scalar(bg_sb[:, 1:2], bg_sb[:, 0:1], -1.0, None, ALU.mult), "bg")
            for b in range(NB):
                dve.wait_ge(s_p0, 2 + b)
                if b >= 2:
                    dve.wait_ge(s_a0, b + 1)
                link(dve.tensor_scalar(rope_sin[:, b % 2, :], psS[:, b % 2, :], modc[:, 1:2], modc[:, 0:1],
                                       ALU.mult, ALU.add), ("hT", b))
                dve.wait_ge(s_a0, 3 + b)
                link(dve.tensor_tensor(hTl[:, b * TB:(b + 1) * TB], rope_sin[:, b % 2, :],
                                       hTh[:, b * TB:(b + 1) * TB], ALU.subtract), ("hTl", b))
            bound = ccol[:, 2:3]
            link(dve.tensor_scalar(ccol[:, 3:4], modc[:, 1:2], -1.0, None, ALU.mult))
            link(dve.tensor_tensor(bound, modc[:, 1:2], ccol[:, 3:4], ALU.max))
            link(dve.tensor_scalar(ccol[:, 3:4], modc[:, 0:1], -1.0, None, ALU.mult))
            link(dve.tensor_tensor(ccol[:, 3:4], modc[:, 0:1], ccol[:, 3:4], ALU.max))
            link(dve.scalar_tensor_tensor(bound, bound, math.sqrt(D), ccol[:, 3:4], ALU.mult, ALU.add))
            link(dve.tensor_scalar(gtmp[:, 0, :], ones[:], bound, None, ALU.mult))
            link(dve.scalar_tensor_tensor(wv_abs, wv_f, -1.0, wv_f, ALU.mult, ALU.max), "bound")
            dve.wait_ge(s_p0, 6)
            link(dve.tensor_reduce(vscale[:, 0:1], psM[:].rearrange("p a b -> p (a b)"), AX.X, ALU.max))
            link(dve.tensor_scalar(vscale[:, 1:2], vscale[:, 0:1], 1e-30, 2.0 ** -15, ALU.max, ALU.mult))
            link(dve.reciprocal(vscale[:, 2:3], vscale[:, 1:2]), "scale")
            dve.wait_ge(s_p0, 7)
            link(dve.tensor_tensor(brow[:, 1, :], psJ[0:1, 0, 0:D], brow[:, 0, :], ALU.add))
            link(dve.tensor_tensor(brow[:, 1, :], brow[:, 1, :], ga[0:1, :], ALU.mult), "brow")
            wo3 = wo_f.rearrange("p (c d) -> p c d", d=D)
            link(dve.scalar_tensor_tensor(wo3, wo3, vscale[:, 1:2], ga[:].unsqueeze(1).to_broadcast([P, 8, D]),
                                          ALU.mult, ALU.mult), "wout")
            dve.wait_ge(s_a0, 7)
            link(dve.tensor_tensor(wv_lo, wv_f, wv_hi, ALU.subtract), "wvl")
            dve.wait_ge(s_a0, 8)
            link(dve.tensor_tensor(wo_lo[:], wo_f, wo_hi[:], ALU.subtract), "wol")
            def rope(g, b):
                t = slice(b * TB, (b + 1) * TB)
                wait(dve, s_proj, g.count(NB, b + 1))
                wait(dve, s_lo, g.count(NB, b + 1 - NB))
                dve.scalar_tensor_tensor(qk[:, t], psJ[:, 0, :], bqk_sb[:, 0, bass.ds(index(g), 1)],
                                         cs[:, 0, t], ALU.add, ALU.mult).then_inc(s_rope, 1)
                wait(dve, s_qk, g.count(NB, b - 1))
                dve.scalar_tensor_tensor(rope_sin[:, b % 2, :], psJ[:, 1, :],
                                         bqk_sb[:, 1, bass.ds(index(g), 1)], cs[:, 1, t],
                                         ALU.add, ALU.mult).then_inc(s_rope, 1)

            def reduce_chunk(g, c):
                qt, k0, w, _ = CHUNKS[c]
                wait(dve, s_mm, g.count(NC, c + 1))
                if c == 0:
                    wait(dve, s_m, g.count(1, 0))
                dve.tensor_reduce(mxp[:, qt, k0 // TB:k0 // TB + 1], chunk_scores(c)[:, 0:w], AX.X,
                                  ALU.max).then_inc(s_red, 1)

            def maxima(g):
                wait(dve, s_red, g.count(NC, NC))
                dve.tensor_reduce(mx[:], mxp[:], AX.X, ALU.max).then_inc(s_m, 1)

            def negate(g):
                wait(dve, s_mt, g.count(1, 1))
                wait(dve, s_mrow[g.plus(-1).par], g.plus(-1).turns(16))
                dve.tensor_scalar(negm[:], psM[0:NT, 0, 0:P], -1.0, SHIFT, ALU.mult,
                                  ALU.add).then_inc(s_neg, 1)

            def normalise(h, b):
                wait(dve, s_pv, h.count(NS, BLOCK_END[b]))
                wait(dve, s_att, h.count(NB, b))
                vals = psV[:, b % 2, 0:TPB * VW].rearrange("p (t w) -> p t w", w=VW)
                dve.reciprocal(rden[:], vals[:, :, DH]).then_inc(s_rden, 1)
                wait(dve, s_rden, h.count(NB, b + 1))
                if b == 0:
                    wait(dve, s_att_st[h.par], h.plus(-2).turns(16))
                dve.tensor_tensor(att[:, h.par, b * TPB:(b + 1) * TPB, :], vals[:, :, 0:DH],
                                  rden[:].unsqueeze(2).to_broadcast([P, TPB, DH]),
                                  ALU.mult).then_inc(s_att, 1)

            def slot(h, attend, maximum, project):
                for j in range(NS):
                    if attend and j + LOW_LEAD < NS and LOW_BY[j + LOW_LEAD] == 0:
                        weights_low(dve, h, j + LOW_LEAD)
                    if attend and j - 1 in BLOCK_END:
                        normalise(h, BLOCK_END.index(j - 1))
                    if project and j - TO_ROPE in PROJ_AT:
                        rope(h.plus(2), PROJ_AT.index(j - TO_ROPE))
                    if maximum:
                        for c in CHUNKS_AT[j]:
                            reduce_chunk(h.plus(1), c)
                        if j == FINAL_AT:
                            maxima(h.plus(1))
                        if j == NEGATE_AT:
                            negate(h.plus(1))
                if maximum:
                    for j in range(LOW_LEAD):
                        if LOW_BY[j] == 0:
                            weights_low(dve, h.plus(1), j)
                if attend:
                    normalise(h, NB - 1)

            dve.wait_ge(s_ld_tab, 16 * len(table_loads))
            for t in range(NT):
                k = t % VR
                dve.wait_ge(s_vcopy_a, t + 1)
                if t >= VR:
                    dve.wait_ge(s_vst[k], 32 * (t // VR))
                dve.scalar_tensor_tensor(prob_lo[:, 2 * k:2 * k + 2, :], (psV if t % 2 else psM)[:],
                                         vscale[:, 2:3], prob_hi[:, 2 * k:2 * k + 2, :], ALU.mult,
                                         ALU.subtract).then_inc(s_vcopy_v, 1)
                if t - 1 in FIRST_PROJ_AT:
                    rope(Head(0, 0), FIRST_PROJ_AT.index(t - 1))

            slots(dve, slot)

            def low_tile(t):
                k = t.par
                wait(dve, s_ah, t.count(1, 1))
                wait(dve, s_y, t.count(1, -1))
                dve.tensor_tensor(qk_lo[:, k * 1024:(k + 1) * 1024],
                                  (psM if k else psS)[:].rearrange("p a b -> p (a b)"),
                                  qk_hi[:, k * 1024:(k + 1) * 1024], ALU.subtract).then_inc(s_al, 1)

            def norm_tile(t):
                k = t.par
                step = [0]

                def then(ins, needed=True):
                    step[0] += 1
                    ins.then_inc(s_x2, 1)
                    if needed:
                        wait(dve, s_x2, t.count(XS, step[0]))

                wait(dve, s_y, t.count(1, 1))
                xcur = xt[:, bass.ds(index(t), 1), :].rearrange("p a b -> p (a b)")
                then(dve.tensor_tensor(x2[:, k, :], psV[:, k, 0:D], xcur, ALU.add))
                then(dve.bn_stats(stats[:, k, :], x2[:, k, :]))
                then(dve.tensor_scalar(xcur, x2[:, k, :], 1.0, None, ALU.mult), False)
                then(dve.bn_aggr(mv[:, k, :], stats[:, k, :]))
                wait(dve, s_sq, t.count(1, 1))
                then(dve.reciprocal(rstd[:, k:k + 1], rstd[:, k:k + 1]))
                wait(dve, s_xT, t.count(1, -1))
                dve.tensor_scalar(xn2[:, k, :], x2[:, k, :], mv[:, k, 0:1], rstd[:, k:k + 1],
                                  ALU.subtract, ALU.mult).then_inc(s_x2, 1)

            def modulate_tile(t):
                wait(dve, s_xT, t.count(1, 1))
                dve.tensor_scalar(h2[:, bass.ds(index(t) * P, P)], psJ[:, t.par, 0:P], modc[:, 4:5],
                                  modc[:, 3:4], ALU.mult, ALU.add).then_inc(s_h2, 1)

            def tile_step(t, turn, project, modulate):
                if turn:
                    low_tile(t)
                if project:
                    norm_tile(t.plus(-1))
                if modulate:
                    modulate_tile(t.plus(-2))

            tiles(dve, tile_step)

            for b in range(NB):
                t = slice(b * TB, (b + 1) * TB)
                dve.wait_ge(s_ez, b + 1)
                dve.tensor_scalar(router[:, t], router[:, t], 1.0, None, ALU.add).then_inc(s_r, 1)
                dve.wait_ge(s_r, 3 * b + 1)
                dve.reciprocal(router[:, t], router[:, t]).then_inc(s_r, 1)
                dve.wait_ge(s_r, 3 * b + 2)
                dve.scalar_tensor_tensor(router[:, t], router[:, t], 0.5, router[:, t], ALU.is_gt,
                                         ALU.mult).then_inc(s_r, 1)

            def hidden_low(tb, i):
                wait(dve, s_hf, tb.count(E * HC, i + 1))
                wait(dve, s_hh, tb.count(E * HC, i + 1))
                wait(dve, s_dn, tb.count(E * HC, i - 3))
                dve.tensor_tensor(hidden(qk_lo, i), prob[:, i % 4, :], hidden(qk_hi, i),
                                  ALU.subtract).then_inc(s_hl, 1)

            def combine(tb, e):
                wait(dve, s_dn, tb.count(E * HC, HC * (e + 1)))
                o, weights = psV[:, (e + 1) % 2, :], spread[tb.par][:, e * TB:(e + 1) * TB]
                if e == 0:
                    wait(dve, s_wb[tb.par], tb.turns(16))
                    wait(dve, s_c, tb.count(XC, 0))
                    dve.tensor_tensor(acc, o, weights, ALU.mult).then_inc(s_c, 1)
                else:
                    wait(dve, s_c, tb.count(XC, 2 * e - 1))
                    dve.tensor_tensor(ctmp, o, weights, ALU.mult).then_inc(s_c, 1)
                    wait(dve, s_c, tb.count(XC, 2 * e))
                    dve.tensor_tensor(acc, acc, ctmp, ALU.add).then_inc(s_c, 1)

            def gate(tb):
                wait(dve, s_o, tb.count(1, 1))
                wait(dve, s_c, tb.count(XC, XC - 2))
                dve.tensor_tensor(acc, acc, psJ[:, 1 - tb.par, :], ALU.add).then_inc(s_c, 1)
                wait(dve, s_c, tb.count(XC, XC - 1))
                wait(dve, s_yt, tb.count(1, 0))
                dve.tensor_scalar(gacc, acc, modc[:, 5:6], None, ALU.mult).then_inc(s_c, 1)

            def output(tb):
                wait(dve, s_yt, tb.count(1, 1))
                xb = xt[:, bass.ds(index(tb) * TPB, TPB), :].rearrange("p a b -> p (a b)")
                dve.tensor_tensor(xb, psJ[:, tb.par, :], xb, ALU.add).then_inc(s_out, 1)

            with dve.Fori(0, NB // 2) as pair:
                for g in range(2 * E * HC + TURN_LAG + 1):
                    if g < 2 * E * HC:
                        hidden_low(Head(pair, g // (E * HC)), g % (E * HC))
                    if g >= 6 and (g - 6) % HC == 0 and (g - 6) // HC < 2 * E:
                        k, e = (g - 6) // HC // E, (g - 6) // HC % E
                        combine(Head(pair, k), e)
                        if e == E - 1:
                            gate(Head(pair, k))
                    if g in TURNS_AT:
                        output(Head(pair, TURNS_AT.index(g)))

        @block.scalar
        def _(act):
            act.wait_ge(s_ld, 16 * len(setup_loads))
            act.activation(ccol[:, 1:2], ccol[:, 0:1], ACT.Exp, scale=-1.0).then_inc(s_a0, 1)
            act.wait_ge(s_ld_tab, 16 * len(table_loads))
            act.copy(Kl[:, 0, :], stage[:, T:2 * T]).then_inc(s_alibi, 1)
            act.wait_ge(s_v0, mark["var"])
            act.activation(rstd[:], rstd[:], ACT.Sqrt).then_inc(s_a0, 1)
            for b in range(NB):
                act.wait_ge(s_v0, mark["hT", b])
                act.copy(hTh[:, b * TB:(b + 1) * TB], rope_sin[:, b % 2, :]).then_inc(s_a0, 1)
            act.copy(wv_hi, wv_f).then_inc(s_a0, 1)
            act.wait_ge(s_v0, mark["wout"])
            act.copy(wo_hi[:], wo_f).then_inc(s_a0, 1)
            def weights_high(g):
                wait(act, s_w[g.par], g.turns(16))
                wait(act, s_proj, g.count(NB, -NB))
                act.copy(wh[:, g.par, :], wf[:, g.par, :]).then_inc(s_wh, 1)

            def high(g, b):
                t = slice(b * TB, (b + 1) * TB)
                wait(act, s_qk, g.count(NB, b + 1))
                if b == 0:
                    wait(act, s_kx[g.par], g.plus(-2).turns(64))
                    wait(act, s_kq[g.par], g.plus(-2).turns(64))
                act.copy(qk_parts[g.par][:, 0, t], qk[:, t]).then_inc(s_hi, 1)

            def exponentiate(h, j):
                w = STEPS[j][3]
                wait(act, s_sc, h.count(NS, j + 1))
                wait(act, s_pv, h.count(NS, j + 1 - NP))
                g, i = (h, j - NF) if j >= NF else (h.plus(-1), j - NF + NS)
                wait(act, s_pl[LOW_BY[i]], g.count(LOW_ALL[LOW_BY[i]], LOW_DONE[i]))
                act.activation(prob[:, j % NF, 0:w], psS[:, j % 2, 0:w], ACT.Exp)
                act.activation(prob_hi[:, j % NP, 0:w], psS[:, j % 2, 0:w], ACT.Exp).then_inc(s_exp, 1)

            def slot(h, attend, maximum, project):
                for j in range(NS):
                    if attend and j + EXP_LEAD < NS:
                        exponentiate(h, j + EXP_LEAD)
                    elif maximum and j + EXP_LEAD >= NS:
                        exponentiate(h.plus(1), j + EXP_LEAD - NS)
                    if project and j == SPLIT_AT:
                        weights_high(h.plus(3))
                    if project and j - TO_HIGH in PROJ_AT:
                        high(h.plus(2), PROJ_AT.index(j - TO_HIGH))

            weights_high(Head(0, 0))
            weights_high(Head(0, 1))
            for t in range(NT):
                act.wait_ge(s_vproj, t + 1)
                k = t % VR
                if t >= VR:
                    act.wait_ge(s_vst[k], 32 * (t // VR))
                act.activation(prob_hi[:, 2 * k:2 * k + 2, :], (psV if t % 2 else psM)[:], ACT.Copy,
                               scale=vscale[:, 2:3]).then_inc(s_vcopy_a, 1)
                if t - 3 in FIRST_PROJ_AT:
                    high(Head(0, 0), FIRST_PROJ_AT.index(t - 3))
            for k in range(VR):
                act.wait_ge(s_vst[k], 32 * NT // VR)
            slots(act, slot)

            def tile_step(t, turn, project, modulate):
                if turn:
                    k = t.par
                    wait(act, s_atT, t.count(1, 1))
                    wait(act, s_y, t.count(1, -1))
                    act.copy(qk_hi[:, k * 1024:(k + 1) * 1024],
                             (psM if k else psS)[:].rearrange("p a b -> p (a b)")).then_inc(s_ah, 1)
                if project:
                    n = t.plus(-1)
                    wait(act, s_x2, n.count(XS, 4))
                    act.activation(rstd[:, n.par:n.par + 1], mv[:, n.par, 1:2], ACT.Sqrt,
                                   bias=eps[:]).then_inc(s_sq, 1)

            tiles(act, tile_step)

            for b in range(NB):
                act.wait_ge(s_z, b + 1)
                act.activation(router[:, b * TB:(b + 1) * TB], psJ[0:E, b % 2, :], ACT.Exp,
                               bias=bg_sb[:, 1:2], scale=-1.0).then_inc(s_ez, 1)

            with act.Fori(0, NB // 2) as pair:
                for k in range(2):
                    tb = Head(pair, k)
                    for i in range(E * HC):
                        u = (psS, psM)[i % 4 // 2][:, i % 2, :]
                        wait(act, s_u, tb.count(E * HC, i + 1))
                        wait(act, s_hl, tb.count(E * HC, i - 3))
                        act.activation(prob[:, i % 4, :], u, ACT.Relu,
                                       bias=b1_sb[:, i:i + 1]).then_inc(s_hf, 1)
                        wait(act, s_dn, tb.count(E * HC, i - 3))
                        act.activation(hidden(qk_hi, i), u, ACT.Relu,
                                       bias=b1_sb[:, i:i + 1]).then_inc(s_hh, 1)

        @block.gpsimd
        def _(pool):
            def projection_weights_low(g):
                wait(pool, s_wh, g.count(1, 1))
                wait(pool, s_w[g.par], g.turns(16))
                wait(pool, s_proj, g.count(NB, -NB))
                pool.tensor_tensor(wl[:, g.par, :], wf[:, g.par, :], wh[:, g.par, :],
                                   ALU.subtract).then_inc(s_wl, 1)

            def sum_block(g, b):
                t = slice(b * TB, (b + 1) * TB)
                wait(pool, s_rope, g.count(2 * NB, 2 * b + 2))
                pool.tensor_tensor(qk[:, t], qk[:, t], rope_sin[:, b % 2, :], ALU.add).then_inc(s_qk, 1)

            def low_block(g, b):
                t = slice(b * TB, (b + 1) * TB)
                wait(pool, s_hi, g.count(NB, b + 1))
                if b == 0:
                    wait(pool, s_kx[g.par], g.plus(-2).turns(64))
                    wait(pool, s_kq[g.par], g.plus(-2).turns(64))
                pool.tensor_tensor(qk_parts[g.par][:, 1, t], qk[:, t], qk_parts[g.par][:, 0, t], ALU.subtract).then_inc(s_lo, 1)

            def slot(h, attend, maximum, project):
                for j in range(NS):
                    if attend and LOW_BY[j]:
                        weights_low(pool, h, j)
                    if project and j == SPLIT_AT:
                        projection_weights_low(h.plus(3))
                    if project and j - TO_SUM in PROJ_AT:
                        sum_block(h.plus(2), PROJ_AT.index(j - TO_SUM))
                    if project and j - TO_LOW in PROJ_AT:
                        low_block(h.plus(2), PROJ_AT.index(j - TO_LOW))

            projection_weights_low(Head(0, 0))
            projection_weights_low(Head(0, 1))
            for b in range(NB):
                sum_block(Head(0, 0), b)
                low_block(Head(0, 0), b)
            slots(pool, slot)

            pool.wait_ge(s_sc, ALL["sc"])
            for n, (loaded, full, high, low) in enumerate(((s_ld_w1, w1_f, k1h, k1l), (s_ld_w2, w2_f, k2h, k2l))):
                pool.wait_ge(loaded, 16)
                pool.tensor_copy(high, full).then_inc(s_fwh, 1)
                pool.wait_ge(s_fwh, n + 1)
                pool.tensor_tensor(low, full, high, ALU.subtract).then_inc(s_fw, 1)

            def tile_step(t, turn, project, modulate):
                if modulate:
                    n = t.plus(-2)
                    c = bass.ds(index(n) * P, P)
                    wait(pool, s_h2, n.count(1, 1))
                    pool.tensor_copy(hTh[:, c], h2[:, c]).then_inc(s_h2h, 1)
                    wait(pool, s_h2h, n.count(1, 1))
                    pool.tensor_tensor(hTl[:, c], h2[:, c], hTh[:, c], ALU.subtract).then_inc(s_h2l, 1)

            tiles(pool, tile_step)

        @block.tensor
        def _(pe):
            pe.wait_ge(s_ld, 16 * len(setup_loads))
            pe.wait_ge(s_v0, mark["silu"])
            for k in range(6):
                pe.matmul(psJ[:, 0, k:k + 1], w_mod[:, k * D:(k + 1) * D], ccol[:, 1:2],
                          start=(k == 0), stop=True, skip_group_check=True)
            pe.matmul(psJ[:, 1, 0:D], gtmp[:, 0, :], w_mod[:, 2 * D:3 * D],
                      start=True, stop=True).then_inc(s_p0, 1)
            for b in range(NB):
                if b >= 2:
                    pe.wait_ge(s_v0, mark["hT", b - 2])
                for t in range(TPB * b, TPB * (b + 1)):
                    pe.wait_ge(s_v0, mark["xn", t])
                    mm = pe.transpose(psS[:, b % 2, (t % TPB) * P:(t % TPB + 1) * P],
                                      qk[:, t * P:(t + 1) * P], eye[:])
                mm.then_inc(s_p0, 1)
            pe.wait_ge(s_v0, mark["bound"])
            for c in range(2):
                mm = pe.matmul(psM[:, c, :], gtmp[:, 0, :], wv_abs[:, c * TB:(c + 1) * TB],
                               start=True, stop=True)
            mm.then_inc(s_p0, 1)
            for c in range(8):
                mm = pe.matmul(psJ[0:1, 0, 0:D], bvc[:, c:c + 1], wo_f[:, c * D:(c + 1) * D],
                               start=(c == 0), stop=(c == 7))
            mm.then_inc(s_p0, 1)
            def project(g, b):
                t = slice(b * TB, (b + 1) * TB)
                if b == 0:
                    wait(pe, s_wh, g.count(1, 1))
                    wait(pe, s_wl, g.count(1, 1))
                wait(pe, s_rope, g.count(2 * NB, 2 * b))
                for half in range(2):
                    o, c = psJ[:, half, :], slice(half * P, (half + 1) * P)
                    pe.matmul(o, wh[:, g.par, c], hTh[:, t], start=True, stop=False)
                    pe.matmul(o, wl[:, g.par, c], hTh[:, t], start=False, stop=False)
                    mm = pe.matmul(o, wh[:, g.par, c], hTl[:, t], start=False, stop=True)
                mm.then_inc(s_proj, 1)

            def max_chunk(g, c, projecting):
                qt, k0, w, diagonal = CHUNKS[c]
                if c == 0:
                    wait(pe, s_kx[g.par], g.turns(64))
                    wait(pe, s_neg, g.count(1, 0))
                if CHUNK_PREV[c] >= 0:
                    wait(pe, s_red, g.count(NC, CHUNK_PREV[c] + 1))
                elif CHUNK_BANK[c] >= 2 and projecting:
                    wait(pe, s_rope, g.plus(1).count(2 * NB, 2 * NB))
                mm = pe.matmul(chunk_scores(c)[:, 0:w], Qx[0:KA, g.par, qt * P:(qt + 1) * P],
                               Kx[0:KA, g.par, k0:k0 + w], start=True, stop=True)
                if diagonal:
                    mm = pe.matmul(chunk_scores(c)[:, w - P:w], eye16[:], maskq[:], start=False, stop=True,
                                   skip_group_check=True)
                mm.then_inc(s_mm, 1)

            def turn_maxima(g):
                wait(pe, s_m, g.count(1, 1))
                pe.transpose(psM[0:NT, 0, 0:P], mx[:], eye[:]).then_inc(s_mt, 1)

            def score(h, j, place_next=False):
                b, kt, q0, w = STEPS[j]
                k = slice(kt * P, (kt + 1) * P)
                if j == 0:
                    wait(pe, s_kq[h.par], h.turns(64))
                    wait(pe, s_mrow[h.par], h.turns(16))
                if j == NS - 1 and place_next:
                    wait(pe, s_lo, h.plus(2).count(NB, NB))
                wait(pe, s_exp, h.count(NS, j - 1))
                o = psS[:, j % 2, 0:w]
                pe.matmul(o, Kx[0:KM, h.par, k], Qx[0:KM, h.par, q0:q0 + w], start=True, stop=False)
                if kt >= TPB * b:
                    pe.matmul(psS[:, j % 2, 0:P], eye16[:], maskk[:], start=False, stop=False,
                              skip_group_check=True)
                mm = pe.matmul(o, Kl[:, h.par, k], Ql[:, h.par, q0:q0 + w], start=False, stop=True)
                mm.then_inc(s_sc, 1)

            def weigh(h, j):
                b, kt, q0, w = STEPS[j]
                if j == 0:
                    wait(pe, s_v[h.par], h.turns(32))
                if kt == 0:
                    wait(pe, s_att, h.count(NB, b - 1))
                wait(pe, s_pl[LOW_BY[j]], h.count(LOW_ALL[LOW_BY[j]], LOW_DONE[j]))
                first = (q0 - b * TB) // P
                for t in range(first, TPB):
                    c = slice((t - first) * P, (t - first + 1) * P)
                    hi, lo = prob_hi[:, j % NP, c], prob_lo[:, j % NP, c]
                    v = v16[:, h.par, kt, :]
                    o = psV[:, b % 2, t * VW:(t + 1) * VW]
                    pe.matmul(o, hi, v[:, 0:VW], start=(kt == 0 and t == 0), stop=False,
                              skip_group_check=True)
                    pe.matmul(o[:, 0:DH], hi, v[:, VW:VW + DH], start=False, stop=False,
                              skip_group_check=True)
                    mm = pe.matmul(o, lo, v[:, 0:VW], start=False, stop=(kt == TPB * b + t),
                                   skip_group_check=True)
                mm.then_inc(s_pv, 1)

            def slot(h, attend, maximum, project_):
                for j in range(NS):
                    if project_ and j in PROJ_AT:
                        project(h.plus(2), PROJ_AT.index(j))
                    if attend:
                        if j + LEAD < NS:
                            score(h, j + LEAD, project_)
                        elif maximum:
                            score(h.plus(1), j + LEAD - NS)
                    if maximum:
                        for c in CHUNKS_AT[j][:1]:
                            max_chunk(h.plus(1), c, project_)
                    if attend:
                        weigh(h, j)
                    if maximum:
                        for c in CHUNKS_AT[j][1:]:
                            max_chunk(h.plus(1), c, project_)
                        if j == TURN_AT:
                            turn_maxima(h.plus(1))
                if maximum and not attend:
                    for j in range(LEAD):
                        score(h.plus(1), j)

            pe.wait_ge(s_v0, mark["wol"])
            for t in range(NT):
                if t >= 2:
                    pe.wait_ge(s_vcopy_a, t - 1)
                    pe.wait_ge(s_vcopy_v, t - 1)
                tt = slice(t * P, (t + 1) * P)
                for c in range(2):
                    cc = slice(c * TB, (c + 1) * TB)
                    o = (psV if t % 2 else psM)[:, c, :]
                    pe.matmul(o, hTh[:, tt], wv_hi[:, cc], start=True, stop=False)
                    pe.matmul(o, hTh[:, tt], wv_lo[:, cc], start=False, stop=False)
                    mm = pe.matmul(o, hTl[:, tt], wv_hi[:, cc], start=False, stop=True)
                mm.then_inc(s_vproj, 1)
                if t in FIRST_PROJ_AT:
                    project(Head(0, 0), FIRST_PROJ_AT.index(t))
            pe.wait_ge(s_vcopy_a, NT)
            pe.wait_ge(s_vcopy_v, NT)
            pe.wait_ge(s_v0, mark["brow"])

            slots(pe, slot)
            pe.wait_ge(s_exp, ALL["exp"])
            pe.wait_ge(s_att, ALL["att"])
            pe.wait_ge(s_neg, ALL["neg"])

            def turn_tile(t):
                k = t.par
                wait(pe, s_at[k], t.turns(16))
                wait(pe, s_al, t.count(1, -1))
                for c in range(8):
                    mm = pe.transpose((psM if k else psS)[:, c // 4, (c % 4) * P:(c % 4 + 1) * P],
                                      qk[:, k * 1024 + c * P:k * 1024 + (c + 1) * P], eye[:])
                mm.then_inc(s_atT, 1)

            def out_tile(t):
                k = t.par
                wait(pe, s_al, t.count(1, 1))
                wait(pe, s_x2, t.count(XS, 1 - 2 * XS))
                o = psV[:, k, 0:D]
                pe.matmul(o, ones[0:1, :], brow[:, 1, :], start=True, stop=False)
                for c in range(8):
                    a = slice(k * 1024 + c * P, k * 1024 + (c + 1) * P)
                    w = slice(c * D, (c + 1) * D)
                    pe.matmul(o, qk_hi[:, a], wo_hi[:, w], start=False, stop=False)
                    pe.matmul(o, qk_hi[:, a], wo_lo[:, w], start=False, stop=False)
                    mm = pe.matmul(o, qk_lo[:, a], wo_hi[:, w], start=False, stop=(c == 7))
                mm.then_inc(s_y, 1)

            def turn_norm(t):
                wait(pe, s_x2, t.count(XS, XS))
                wait(pe, s_h2, t.count(1, -1))
                pe.transpose(psJ[:, t.par, 0:P], xn2[:, t.par, :], eye[:]).then_inc(s_xT, 1)

            def tile_step(t, turn, project_, modulate):
                if turn:
                    turn_tile(t)
                if project_:
                    out_tile(t.plus(-1))
                if modulate:
                    turn_norm(t.plus(-2))

            tiles(pe, tile_step)

            pe.wait_ge(s_h2, NT + CREDIT)
            for b in range(NB):
                if b >= 2:
                    pe.wait_ge(s_ez, b - 1)
                pe.matmul(psJ[0:E, b % 2, :], wg_sb[:], h2[:, b * TB:(b + 1) * TB],
                          start=True, stop=True).then_inc(s_z, 1)
            pe.wait_ge(s_ez, NB)
            pe.wait_ge(s_x2, XS * NT + CREDIT)
            pe.wait_ge(s_fw, 2)
            pe.wait_ge(s_h2l, NT + CREDIT)

            def hidden_scores(tb, i):
                t = bass.ds(index(tb) * TB, TB)
                w = slice(i * P, (i + 1) * P)
                o = (psS, psM)[i % 4 // 2][:, i % 2, :]
                wait(pe, s_hh, tb.count(E * HC, i - 3))
                pe.matmul(o, k1h[:, w], hTh[:, t], start=True, stop=False)
                pe.matmul(o, k1l[:, w], hTh[:, t], start=False, stop=False)
                pe.matmul(o, k1h[:, w], hTl[:, t], start=False, stop=True).then_inc(s_u, 1)

            def expert_out(tb, i):
                e, c = i // HC, i % HC
                w = slice(i * P, (i + 1) * P)
                o = psV[:, (e + 1) % 2, :]
                if c == 0:
                    wait(pe, s_c, tb.count(XC, -5 if e == 0 else -3 if e == 1 else max(1, 2 * e - 4)))
                wait(pe, s_hl, tb.count(E * HC, i + 1))
                pe.matmul(o, k2h[:, w], hidden(qk_hi, i), start=(c == 0), stop=False)
                pe.matmul(o, k2l[:, w], hidden(qk_hi, i), start=False, stop=False)
                mm = pe.matmul(o, k2h[:, w], hidden(qk_lo, i), start=False, stop=(c == HC - 1))
                mm.then_inc(s_dn, 1)
                return mm

            def output_biases(tb):
                pe.wait_ge(s_r, 3 * NB)
                wait(pe, s_out, tb.count(1, 0))
                pe.matmul(psJ[:, 1 - tb.par, :], b2_sb[:], router[:, bass.ds(index(tb) * TB, TB)],
                          start=True, stop=True).then_inc(s_o, 1)

            def turn_sum(tb):
                wait(pe, s_c, tb.count(XC, XC))
                for t in range(TPB):
                    mm = pe.transpose(psJ[:, tb.par, t * P:(t + 1) * P], gacc[:, t * P:(t + 1) * P], eye[:])
                mm.then_inc(s_yt, 1)

            with pe.Fori(0, NB // 2) as pair:
                for g in range(2 * E * HC + TURN_LAG + 1):
                    if g < 2 * E * HC:
                        hidden_scores(Head(pair, g // (E * HC)), g % (E * HC))
                    if 3 <= g < 2 * E * HC + 3:
                        expert_out(Head(pair, (g - 3) // (E * HC)), (g - 3) % (E * HC))
                    if g % (E * HC) == E * HC // 2:
                        output_biases(Head(pair, g // (E * HC)))
                    if g in TURNS_AT:
                        turn_sum(Head(pair, TURNS_AT.index(g)))

        @block.sync
        def _(sp):
            def fixed(value):
                return value if isinstance(value, int) else sp.snap(value)

            for s in looped:
                sp.sem_inc(s, CREDIT)
            for dst, src in setup_loads:
                sp.dma_start(dst, src).then_inc(s_ld, 16)
            for dst, src in table_loads:
                sp.dma_start(dst, src).then_inc(s_ld_tab, 16)
            def load_weights(g):
                n = fixed(index(g))
                wait(sp, s_wl, g.count(1, -1))
                sp.dma_start(wf[:, g.par, :], wqk[bass.ds(n, 1)].rearrange("a p c -> p (a c)")
                             ).then_inc(s_w[g.par], 16)

            def load_values(g):
                n = fixed(index(g) + V_AT)
                wait(sp, s_pv, g.count(NS, -NS))
                for part in range(2):
                    sp.dma_start(v16[:, g.par, :, part * VW:part * VW + DH],
                                 v_dram[:, :, part, bass.ds(n, 1)].rearrange("p t a d -> p (t a) d")
                                 ).then_inc(s_v[g.par], 16)

            def place(g, attend):
                k = g.par
                n = fixed(index(g))
                if attend:
                    wait(sp, s_sc, g.count(NS, -NS))
                else:
                    wait(sp, s_lo, g.count(NB, NB))
                for rows, side in ((Kx, 0), (Qx, 1)):
                    sp.dma_start(rows[DH:KA, k, :].bitcast(F32),
                                 ext_dram[bass.ds(n, 1), side].rearrange("a r t -> r (a t)").bitcast(F32)).then_inc(s_kx[k], 16)
                hi, lo = qk_parts[k][:, 0, :], qk_parts[k][:, 1, :]
                for done, dst, src in ((s_kx, Kx[0:DH, k, :], hi[DH:P, :]), (s_kx, Qx[0:DH, k, :], hi[0:DH, :]),
                                       (s_kq, Kl[0:DH, k, :], lo[DH:P, :]), (s_kq, Kl[DH:P, k, :], hi[DH:P, :]),
                                       (s_kq, Ql[0:DH, k, :], hi[0:DH, :]), (s_kq, Ql[DH:P, k, :], lo[0:DH, :])):
                    sp.dma_start(dst.bitcast(F32), src.bitcast(F32)).then_inc(done[k], 16)

            def slot(h, attend, maximum, project):
                if attend and not project:
                    if maximum:
                        sp.wait_ge(s_rope, ALL["rope"])
                        sp.dma_start(w1_f, w1).then_inc(s_ld_w1, 16)
                    else:
                        sp.wait_ge(s_kx[1], 64 * H // 2 + CREDIT)
                        sp.wait_ge(s_kq[1], 64 * H // 2 + CREDIT)
                        sp.dma_start(w2_f, w2).then_inc(s_ld_w2, 16)
                if project:
                    load_weights(h.plus(3))
                if maximum:
                    load_values(h.plus(1))
                    g = h.plus(1)
                    wait(sp, s_neg, g.count(1, 1))
                    sp.dma_start(Qx[KA:KM, g.par, :].bitcast(F32), negm[:].bitcast(F32)).then_inc(s_mrow[g.par], 16)
                if project:
                    place(h.plus(2), attend)
                if attend:
                    n = fixed(index(h) * DH)
                    wait(sp, s_att, h.count(NB, NB))
                    sp.dma_start(att_dram.rearrange("(n p) c -> p n c", p=P)[:, :, bass.ds(n, DH)],
                                 att[:, h.par, :, :]).then_inc(s_att_st[h.par], 16)

            load_weights(Head(0, 0))
            load_weights(Head(0, 1))
            sp.wait_ge(s_alibi, 1)
            sp.dma_start(ext_dram.rearrange("h s r t -> (h s r) t").bitcast(F32),
                         Kl[:, 0, :].bitcast(F32)).then_inc(s_alibi_st, 16)
            for t in range(NT):
                sp.wait_ge(s_vcopy_a, t + 1)
                sp.wait_ge(s_vcopy_v, t + 1)
                k = t % VR
                for part, tile in enumerate((prob_hi, prob_lo)):
                    sp.dma_start(v_dram[:, t, part, V_AT:].rearrange("p h d -> p (h d)"),
                                 tile[:, 2 * k:2 * k + 2, :].rearrange("p a b -> p (a b)")
                                 ).then_inc(s_vst[k], 16)
            for k in range(VR):
                sp.wait_ge(s_vst[k], 32 * NT // VR)
            sp.wait_ge(s_alibi_st, 16)
            sp.wait_ge(s_v0, mark["wol"])
            place(Head(0, 0), False)
            slots(sp, slot)
            for par in range(2):
                sp.wait_ge(s_att_st[par], 16 * H // 2 + CREDIT)
            sp.wait_ge(s_lo, ALL["lo"])

            with sp.Fori(0, NT // 2) as pair:
                for k in range(2):
                    t = Head(pair, k)
                    n = fixed(index(t) * P)
                    wait(sp, s_atT, t.count(1, -1))
                    sp.dma_start(qk[:, k * 1024:(k + 1) * 1024],
                                 att_dram[bass.ds(n, P), :]).then_inc(s_at[k], 16)

            sp.wait_ge(s_r, 3 * NB)
            sp.dma_start(wt_dram, router).then_inc(s_wt_st, 16)
            sp.wait_ge(s_wt_st, 16)
            sp.wait_ge(s_fw, 2)
            out_t = out.rearrange("(n p) d -> p n d", p=P)
            with sp.Fori(0, NB // 2) as pair:
                for k in range(2):
                    tb = Head(pair, k)
                    n = fixed(index(tb) * TB)
                    wait(sp, s_c, tb.count(XC, 2 * (E - 1) - 2 * XC))
                    sp.dma_start(spread[k].rearrange("p (e t) -> p e t", e=E),
                                 wt_dram[:, bass.ds(n, TB)].partition_broadcast(P)
                                 ).then_inc(s_wb[k], 16)
                for k in range(2):
                    tb = Head(pair, k)
                    n = bass.ds(fixed(index(tb) * TPB), TPB)
                    wait(sp, s_out, tb.count(1, 1))
                    sp.dma_start(out_t[:, n, :], xt[:, n, :]).then_inc(s_st, 16)
            sp.wait_ge(s_st, 16 * NB)


def slopes():
    start = 2.0 ** (-8.0 / H)
    return [start * start ** i for i in range(H)]


def kernel(**inputs):
    import numpy as np
    import concourse.bacc as bacc
    from concourse.bass_utils import run_bass_kernel_spmd

    a = {k: np.asarray(v) for k, v in inputs.items()}
    f = np.float32
    inv = f(1.0) / (f(10000.0) ** (np.arange(0, DH, 2, dtype=f) / f(DH)))
    angle = np.outer(inv, np.arange(T, dtype=f)).astype(f).astype(np.float64)
    cos, sin = np.cos(angle), np.sin(angle)
    scale = 1.0 / np.sqrt(3.0 * DH)
    cos2, sin2 = np.concatenate([cos, cos]), np.concatenate([-sin, sin])
    cossin = np.stack([np.concatenate([cos2 * scale, cos2]), np.concatenate([sin2 * scale, sin2])], 1).astype(f)
    pos, one = np.arange(T, dtype=f), np.ones(T, f)
    c = (np.array(slopes()).astype(f) * f(8.0)).astype(f)
    c_hi = (c.view(np.uint32) & np.uint32(0xFFFFF000)).view(f)
    c_lo = c - c_hi
    ext = np.stack([np.stack([np.stack([pos, hi * one, pos, lo * one]), np.stack([hi * one, -pos, lo * one, -pos])])
                    for hi, lo in zip(c_hi, c_lo)])
    i, j = np.meshgrid(np.arange(P), np.arange(P), indexing="ij")
    consts = np.stack([(i == j) * 1.0, (j > i) * -1e9, (i > j) * -1e9], 1).astype(f)

    wq = a["L0_attn_w_qkv"]
    bq = a["L0_attn_b_qkv"]
    swap = np.r_[32:64, 0:32, 96:128, 64:96]
    arrays = {
        "x": a["L0_attn_x"].reshape(T, D),
        "c_col": a["L0_c"].reshape(D, 1),
        "wmod": a["L0_wmod"],
        "cossin": cossin, "ext": ext, "consts": consts,
        "wqk": np.concatenate([wq[:, :, 0:128], wq[:, :, swap]], 2).transpose(1, 0, 2)[np.r_[0:H, H - 1]],
        "bqk": np.stack([bq[:, 0:128].T, bq[:, swap].T], 1),
        "wv": wq[:, :, 128:192].reshape(D, H * DH),
        "bv": bq[:, 128:192].reshape(8, P).T,
        "wout": a["L0_attn_w_out"].reshape(8, P, D).transpose(1, 0, 2).reshape(P, 8 * D),
        "bout": a["L0_attn_b_out"].reshape(1, D),
        "wg": a["L0_ffn_Wg"],
        "bg": a["L0_ffn_bg"].reshape(E, 1),
        "w1": a["L0_ffn_W1"].transpose(1, 0, 2).reshape(D, E * HID),
        "b1": a["L0_ffn_b1"].reshape(E * HC, P).T,
        "w2": a["L0_ffn_W2"].reshape(E, HC, P, D).transpose(2, 0, 1, 3).reshape(P, E * HC * D),
        "b2": a["L0_ffn_b2"],
    }
    nc = bacc.Bacc("TRN2", target_bir_lowering=False, num_devices=1)
    arrays = {f"in_{k}": np.ascontiguousarray(v) for k, v in arrays.items()}
    args = {k[3:]: nc.dram_tensor(k, v.shape, mybir.dt.from_np(v.dtype), kind="ExternalInput").ap()
            for k, v in arrays.items()}
    args["out"] = nc.dram_tensor("out", (T, D), F32, kind="ExternalOutput").ap()
    build(nc, **args)
    r = run_bass_kernel_spmd(nc, [arrays], core_ids=[0])
    return r.results[0]["out"].reshape(1, T, D)
```
